# Optimizing a Trainium2 kernel written in Bass

```python
import numpy as np
import jax
import jax.numpy as jnp

def _softmax(x, axis=-1):
    return jax.nn.softmax(x, axis=axis)

def _gelu(x):
    return jax.nn.gelu(x, approximate=True)

def _silu(x):
    return jax.nn.silu(x)

def _sigmoid(x):
    return jax.nn.sigmoid(x)

def _layernorm(x, axis=-1, eps=1e-05):
    m = jnp.mean(x, axis=axis, keepdims=True)
    v = jnp.var(x, axis=axis, keepdims=True)
    return (x - m) / jnp.sqrt(v + eps)

def _scatter_add(tgt, idx, src, axis=0):
    return tgt.at[idx].add(src)

def _segment_sum(src, seg, n):
    return jax.ops.segment_sum(src, seg, n)
kernel_name = 'mk_adaln_d1_jaxref_r8_28a4c7'

def setup_inputs(seed: int=0):
    np.random.seed(seed)
    _w = jnp.asarray

    def _L0_attn_setup():
        import jax, jax.numpy as jnp
        import numpy as np
        EMBED_DIM = 256
        NUM_HEADS = 16
        HEAD_DIM = EMBED_DIM // NUM_HEADS
        KV_C = 64
        Q_C = 192
        B, S = (2, 256)
        SCALE = 1.0 / np.sqrt(HEAD_DIM)
        key = jax.random.key(seed)
        ks = jax.random.split(key, 6)
        init = lambda k, shape: jax.random.normal(k, shape, dtype=jnp.float32) / np.sqrt(shape[1])
        return {'x': jax.random.normal(ks[0], (B, S, EMBED_DIM), dtype=jnp.float32), 'w_dq': init(ks[1], (Q_C, EMBED_DIM)), 'w_uq': init(ks[2], (NUM_HEADS * HEAD_DIM, Q_C)), 'w_dkv': init(ks[3], (KV_C, EMBED_DIM)), 'w_ukv': init(ks[4], (2 * NUM_HEADS * HEAD_DIM, KV_C)), 'w_out': init(ks[5], (EMBED_DIM, EMBED_DIM))}
    _L0_attn_in = _L0_attn_setup()

    def _L0_ffn_setup():
        import jax, jax.numpy as jnp
        import numpy as np
        H = 256
        key = jax.random.key(seed)
        ks = jax.random.split(key, 10)
        s = 1.0 / np.sqrt(H)
        x = jax.random.normal(ks[0], (4, 256, H), dtype=jnp.float32)
        Wg = jax.random.uniform(ks[1], (2, H), jnp.float32, -s, s)
        W0a = jax.random.uniform(ks[2], (2 * H, H), jnp.float32, -s, s)
        b0a = jax.random.uniform(ks[3], (2 * H,), jnp.float32, -s, s)
        W0b = jax.random.uniform(ks[4], (H, 2 * H), jnp.float32, -s, s)
        b0b = jax.random.uniform(ks[5], (H,), jnp.float32, -s, s)
        W1a = jax.random.uniform(ks[6], (2 * H, H), jnp.float32, -s, s)
        b1a = jax.random.uniform(ks[7], (2 * H,), jnp.float32, -s, s)
        W1b = jax.random.uniform(ks[8], (H, 2 * H), jnp.float32, -s, s)
        b1b = jax.random.uniform(ks[9], (H,), jnp.float32, -s, s)
        return {'x': x, 'Wg': Wg, 'W0a': W0a, 'b0a': b0a, 'W0b': W0b, 'b0b': b0b, 'W1a': W1a, 'b1a': b1a, 'W1b': W1b, 'b1b': b1b}
    _L0_ffn_in = _L0_ffn_setup()
    _L0_c = _w((lambda *s: np.random.randn(*s).astype(np.float32) * 0.05)(16, 256))
    _L0_wmod = _w((lambda *s: np.random.randn(*s).astype(np.float32) * 0.05)(256, 6 * 256) * 256 ** (-0.5))
    _d = {'L0_attn_x': _L0_attn_in['x'], 'L0_attn_w_dq': _L0_attn_in['w_dq'], 'L0_attn_w_uq': _L0_attn_in['w_uq'], 'L0_attn_w_dkv': _L0_attn_in['w_dkv'], 'L0_attn_w_ukv': _L0_attn_in['w_ukv'], 'L0_attn_w_out': _L0_attn_in['w_out'], 'L0_ffn_Wg': _L0_ffn_in['Wg'], 'L0_ffn_W0a': _L0_ffn_in['W0a'], 'L0_ffn_b0a': _L0_ffn_in['b0a'], 'L0_ffn_W0b': _L0_ffn_in['W0b'], 'L0_ffn_b0b': _L0_ffn_in['b0b'], 'L0_ffn_W1a': _L0_ffn_in['W1a'], 'L0_ffn_b1a': _L0_ffn_in['b1a'], 'L0_ffn_W1b': _L0_ffn_in['W1b'], 'L0_ffn_b1b': _L0_ffn_in['b1b'], 'L0_c': _L0_c, 'L0_wmod': _L0_wmod}
    _x0 = _d['L0_attn_x']
    _d['L0_attn_x'] = jax.random.normal(jax.random.fold_in(jax.random.key(seed), 1), (16, 256, 256), dtype=_x0.dtype)
    del _x0
    return _d

def reference(L0_attn_x, L0_attn_w_dq, L0_attn_w_uq, L0_attn_w_dkv, L0_attn_w_ukv, L0_attn_w_out, L0_ffn_Wg, L0_ffn_W0a, L0_ffn_b0a, L0_ffn_W0b, L0_ffn_b0b, L0_ffn_W1a, L0_ffn_b1a, L0_ffn_W1b, L0_ffn_b1b, L0_c, L0_wmod):

    def _L0_attn_ref(x, w_dq, w_uq, w_dkv, w_ukv, w_out):
        import jax, jax.numpy as jnp
        import numpy as np
        EMBED_DIM = 256
        NUM_HEADS = 16
        HEAD_DIM = EMBED_DIM // NUM_HEADS
        KV_C = 64
        Q_C = 192
        B, S = (2, 256)
        SCALE = 1.0 / np.sqrt(HEAD_DIM)
        b, s, _ = x.shape
        q = x @ w_dq.T @ w_uq.T
        kv = x @ w_dkv.T @ w_ukv.T
        k, v = jnp.split(kv, 2, axis=-1)
        q = q.reshape(b, s, NUM_HEADS, HEAD_DIM).transpose(0, 2, 1, 3)
        k = k.reshape(b, s, NUM_HEADS, HEAD_DIM).transpose(0, 2, 1, 3)
        v = v.reshape(b, s, NUM_HEADS, HEAD_DIM).transpose(0, 2, 1, 3)
        attn = jnp.einsum('bhqd,bhkd->bhqk', q, k) * SCALE
        mask = jnp.triu(jnp.full((s, s), -jnp.inf, dtype=attn.dtype), k=1)
        attn = attn + mask
        attn = jax.nn.softmax(attn.astype(jnp.float32), axis=-1).astype(q.dtype)
        out = jnp.einsum('bhqk,bhkd->bhqd', attn, v)
        out = out.transpose(0, 2, 1, 3).reshape(b, s, NUM_HEADS * HEAD_DIM)
        return out @ w_out.T

    def _L0_ffn_ref(x, Wg, W0a, b0a, W0b, b0b, W1a, b1a, W1b, b1b):
        import jax, jax.numpy as jnp
        import numpy as np
        H = 256
        scores = jax.nn.softmax(jnp.einsum('bsh,eh->bse', x, Wg), axis=-1)
        top_expert = jnp.argmax(scores, axis=-1)
        h0 = jax.nn.gelu(jnp.einsum('bsh,fh->bsf', x, W0a) + b0a, approximate=False)
        out0 = jnp.einsum('bsf,hf->bsh', h0, W0b) + b0b
        h1 = jax.nn.relu(jnp.einsum('bsh,fh->bsf', x, W1a) + b1a)
        out1 = jnp.einsum('bsf,hf->bsh', h1, W1b) + b1b
        mask0 = (top_expert == 0).astype(x.dtype)[..., None]
        return out0 * mask0 + out1 * (1.0 - mask0)
    x = L0_attn_x
    mod = (_silu(L0_c) @ L0_wmod).reshape(L0_c.shape[0], 6, 1, -1)
    sa, ca, ga, sb, cb, gb = (mod[:, 0], mod[:, 1], mod[:, 2], mod[:, 3], mod[:, 4], mod[:, 5])
    ga = (2 * (ga >= 0) - 1) * jnp.maximum(jnp.abs(ga), 0.25)
    gb = (2 * (gb >= 0) - 1) * jnp.maximum(jnp.abs(gb), 0.25)
    h = _layernorm(x, axis=-1) * (1 + ca) + sa
    x = x + ga * _L0_attn_ref(h, L0_attn_w_dq, L0_attn_w_uq, L0_attn_w_dkv, L0_attn_w_ukv, L0_attn_w_out)
    h = _layernorm(x, axis=-1) * (1 + cb) + sb
    x = x + gb * _L0_ffn_ref(h, L0_ffn_Wg, L0_ffn_W0a, L0_ffn_b0a, L0_ffn_W0b, L0_ffn_b0b, L0_ffn_W1a, L0_ffn_b1a, L0_ffn_W1b, L0_ffn_b1b)
    return x

_drawn_inputs = setup_inputs


def setup_inputs(seed=0):
    import zlib

    import numpy as np

    out = dict(_drawn_inputs(seed))
    spreads = {}
    factors = {'L0_ffn_b0a': 8.0, 'L0_ffn_b0b': 8.0, 'L0_ffn_b1a': 8.0, 'L0_ffn_b1b': 8.0}
    for name, (base, spread) in spreads.items():
        noise = np.random.default_rng([zlib.crc32(name.encode()), seed]).standard_normal(out[name].shape)
        drawn = base * np.exp(spread * noise) if base else spread * noise
        out[name] = jnp.asarray(drawn.astype(out[name].dtype))
    for name, factor in factors.items():
        out[name] = (out[name] * factor).astype(out[name].dtype)
    return out
```

```python
from contextlib import ExitStack

import concourse.bass as bass
from concourse import mybir

ALU = mybir.AluOpType
ACT = mybir.ActivationFunctionType
AX_X = mybir.AxisListType.X
F32 = mybir.dt.float32
F32R = mybir.dt.float32r
BF16 = mybir.dt.bfloat16

P = 128
EPS = 1e-5
NEG = -3.0e38
LEAST_GATE = 0.25
SPLITS = ((0, 0), (0, 1), (0, 2), (1, 0), (1, 1), (2, 0))


def wait(eng, sem, value):
    if not isinstance(value, int) or value > 0:
        eng.wait_ge(sem, value)


class Batch:

    def __init__(self, i, k, batches):
        self.n, self.half, self.parity = 2 * i + k, i + k // 2, k % 2
        self.static = isinstance(i, int)
        self.off = self.static and not 0 <= self.n < batches
        self.first = self.static and self.n == 0


def wait_alone(eng):
    eng.nop(nofuse=True)


def block_kernel(nc, x, w_dq, w_uqT, w_dkvT, w_ukT, w_uvT, w_outT, wgT, waT, wbT, ba, bb, cT, wmod, out):
    NB, S, D = x.shape
    QC = w_dq.shape[0]
    C = w_dkvT.shape[1]
    HD = 16
    NH = D // HD
    KT = D // P
    TT = S // P
    F = waT.shape[1]
    FT = F // P
    SCALE = float(HD) ** -0.5
    QROWS = QC // 2
    NSPLIT = len(SPLITS)
    R = NSPLIT * HD
    RM = R + 3
    G8 = P // HD
    assert S == 2 * P and D == 2 * P and C == 64 and NH == 16 and F == 4 * D and NB % 2 == 0 and NB >= 8
    CH = 6
    LOADS = 16 * NSPLIT

    ctx = ExitStack()

    def sb(name, shape, dt=F32):
        return ctx.enter_context(nc.sbuf_tensor(name, shape, dt))

    def psum(name):
        return ctx.enter_context(nc.psum_tensor(name, [P, 512], F32))

    def sem(name):
        return ctx.enter_context(nc.semaphore(name))

    with ctx:
        ps_s = ctx.enter_context(nc.psum_tensor("ps_s", [P, 1024], F32))
        ps_t = ctx.enter_context(nc.psum_tensor("ps_t", [P, 1024], F32))
        ps_o = psum("ps_o")
        ps_a, ps_b, ps_c = psum("ps_a"), psum("ps_b"), psum("ps_c")

        xs = sb("xs", [P, NB * TT, D])
        wq = [sb(f"wq{i}", [P, KT, D], F32R) for i in range(2)]
        wdkv = [sb(f"wdkv{i}", [P, KT, 2 * C], F32R) for i in range(2)]
        wuk = [sb(f"wuk{i}", [P, D], F32R) for i in range(2)]
        wuv = [sb(f"wuv{i}", [P, D], F32R) for i in range(2)]
        wout = [sb(f"wout{i}", [P, KT, D], F32R) for i in range(2)]
        wg = [sb(f"wg{i}", [P, KT, 2], F32R) for i in range(2)]
        wa = [sb(f"wa{i}", [P, KT, F], F32R) for i in range(2)]
        wb = [sb(f"wb{i}", [P, FT, D], F32R) for i in range(2)]
        bias_a = sb("bias_a", [P, FT])
        bias_b = sb("bias_b", [P, 2 * D], F32R)
        ones_r = sb("ones_r", [P, P], F32R)
        ident = sb("ident", [P, P])
        ident_b = sb("ident_b", [P, P], BF16)
        mask_b = sb("mask_b", [P, P], BF16)
        neg_half = sb("neg_half", [P, TT])
        modT = sb("modT", [P, NB, 8])
        z1 = sb("z1", [P, TT, D])
        h32 = sb("h32", [P, KT, S])
        h_hi, h_lo = sb("h_hi", [P, KT, S], F32R), sb("h_lo", [P, KT, S], F32R)
        parts_q, parts_k = sb("parts_q", [P, 3, KT * S], BF16), sb("parts_k", [P, 3, KT * S], BF16)
        rest_q, rest_k = sb("rest_q", [P, KT * S]), sb("rest_k", [P, KT * S])
        ckv = sb("ckv", [P, S], F32R)
        v = [sb(f"v{i}", [P, TT, NH, HD + 1]) for i in range(2)]
        qs = [sb(f"qs{i}", [RM, NH, S], BF16) for i in range(2)]
        ks = [sb(f"ks{i}", [RM, NH, S], BF16) for i in range(2)]
        mx = sb("mx", [P, TT, NH])
        mx_parts = sb("mx_parts", [P, TT, 3, NH], BF16)
        mx_rest = sb("mx_rest", [P, TT, NH])
        mx_rows = sb("mx_rows", [3 * NH, S], BF16)
        p0 = sb("p0", [P, NH, S])
        p1 = sb("p1", [P, NH, P])
        oT = sb("oT", [P, 4, S])
        rden = sb("rden", [P, TT, NH])
        attn = sb("attn", [P, TT, D])
        a_hi, a_lo = sb("a_hi", [P, KT, S], F32R), sb("a_lo", [P, KT, S], F32R)
        gated = sb("gated", [P, TT, D])
        z2 = sb("z2", [P, TT, D])
        g32 = sb("g32", [P, KT, S])
        g_hi, g_lo = sb("g_hi", [P, KT, S], F32R), sb("g_lo", [P, KT, S], F32R)
        logit_rows = sb("logit_rows", [2, S])
        logits = sb("logits", [P, TT, 2])
        first = [sb(f"first{i}", [P, TT]) for i in range(2)]
        second = [sb(f"second{i}", [P, TT]) for i in range(2)]
        hid32 = sb("hid32", [P, 2, 2, S])
        hid_hi, hid_lo = sb("hid_hi", [P, FT, S], F32R), sb("hid_lo", [P, FT, S], F32R)
        y = sb("y", [P, TT, D])
        gates = [sb(f"gates{i}", [P, 2, D]) for i in range(2)]
        ln_st = [sb(f"ln_st{i}", [P, TT, 6]) for i in range(2)]
        ln_mv = [sb(f"ln_mv{i}", [P, TT, 2]) for i in range(2)]
        ln_ve = [sb(f"ln_ve{i}", [P, TT]) for i in range(2)]
        ln_rs = [sb(f"ln_rs{i}", [P, TT]) for i in range(2)]
        gates_dram = nc.dram_tensor("gates_scratch", (NB, 2 * D), F32, kind="Internal").ap()

        raw = p0[:].rearrange("p h s -> p (h s)")
        cuts = [KT * 6 * D, KT * D, KT * 2 * C, D]
        at = [sum(cuts[:i]) for i in range(5)]
        wmod_raw = raw[:, at[0]:at[1]].rearrange("p (k f) -> p k f", k=KT)
        wout_raw = raw[:, at[1]:at[2]].rearrange("p (k f) -> p k f", k=KT)
        wdkv_raw = raw[:, at[2]:at[3]].rearrange("p (k f) -> p k f", k=KT)
        wuk_raw = raw[:, at[3]:at[4]]
        wa_raw = p1[:].rearrange("p h s -> p (h s)").rearrange("p (k f) -> p k f", k=KT)
        wb_raw = [hid32[:].rearrange("p a b s -> p (a b) s"), oT[:]]
        wdq_raw, wuq_raw, wuv_raw, wg_raw = z2[:], attn[:], gated[:, 0, :], logits[:]
        bb_raw = v[1][:].rearrange("p t h e -> p (t h e)")[0:2, 0:2 * D]
        cT_raw, c_silu = mx[:], mx_rest[:]
        modrow = [g32[:].rearrange("p k s -> p (k s)")[0:NB], y[:].rearrange("p k s -> p (k s)")[0:NB]]
        clamped, sign = [g[:].rearrange("p g d -> p (g d)")[0:NB] for g in gates]

        x_in0, x_in1, weights_in, mod_in, ffn_in, silu_ready, mod_done, modrow_ready, clamp_ready, gates_stored, modt_done, modt_ready = (sem(n) for n in
            "x_in0 x_in1 weights_in mod_in ffn_in silu_ready mod_done modrow_ready clamp_ready gates_stored modt_done modt_ready".split())
        wq_done, w_hi, w_lo, bias_lo_in, blank, consts_ready, mask_blank = (sem(n) for n in
            "wq_done w_hi w_lo bias_lo_in blank consts_ready mask_blank".split())
        gates_in0, gates_in1, stored0, stored1, q_in0, q_in1, k_in0, k_in1, maxrows_in = (sem(n) for n in
            "gates_in0 gates_in1 stored0 stored1 q_in0 q_in1 k_in0 k_in1 maxrows_in".split())
        z1_ready, t1_done, h32_ready, h_hi_ready, h_lo_ready = (sem(n) for n in
            "z1_ready t1_done h32_ready h_hi_ready h_lo_ready".split())
        q_done, q1_ready, qr_ready, q2_ready, q3_ready, k_done, k1_ready, kr_ready, k2_ready, k3_ready = (sem(n) for n in
            "q_done q1_ready qr_ready q2_ready q3_ready k_done k1_ready kr_ready k2_ready k3_ready".split())
        ckv_done, ckv_hi_ready, ckv_ready, v_done, v_ready = (sem(n) for n in
            "ckv_done ckv_hi_ready ckv_ready v_done v_ready".split())
        s_done, max_done, max_split, mt_done, mt_ready, st_done, exp_done, masked, pv_done, o_ready = (sem(n) for n in
            "s_done max_done max_split mt_done mt_ready st_done exp_done masked pv_done o_ready".split())
        ot_done, rden_ready, attn_ready, at_done, a_hi_ready, a_lo_ready, op_done, gated_ready, x1_ready = (sem(n) for n in
            "ot_done rden_ready attn_ready at_done a_hi_ready a_lo_ready op_done gated_ready x1_ready".split())
        z2_ready, t2_done, g32_ready, g_hi_ready, g_lo_ready, gate_done, logit_rows_ready, gate_turned, logits_ready, first_ready, choice_ready = (sem(n) for n in
            "z2_ready t2_done g32_ready g_hi_ready g_lo_ready gate_done logit_rows_ready gate_turned logits_ready first_ready choice_ready".split())
        up_done, gelu_done, relu_done, hid_hi_ready, lo_gelu_ready, lo_relu_ready = (sem(n) for n in
            "up_done gelu_done relu_done hid_hi_ready lo_gelu_ready lo_relu_ready".split())
        dn_done, second_ready, y_ready, scaled, out_ready = (sem(n) for n in
            "dn_done second_ready y_ready scaled out_ready".split())
        st1, mv1, ve1, rs1, st2, mv2, ve2, rs2 = (sem(n) for n in
            "st1 mv1 ve1 rs1 st2 mv2 ve2 rs2".split())
        x_in, gates_in, stored = (x_in0, x_in1), (gates_in0, gates_in1), (stored0, stored1)
        q_in, k_in = (q_in0, q_in1), (k_in0, k_in1)

        splits = [(wdkv[0][:], wdkv[1][:], wdkv_raw), (wuk[0][:], wuk[1][:], wuk_raw), (wuv[0][:], wuv[1][:], wuv_raw),
                  (wq[0][:], wq[1][:], ps_c[:].rearrange("p (k f) -> p k f", k=KT)), (wout[0][:], wout[1][:], wout_raw),
                  (wa[0][:], wa[1][:], wa_raw), (wb[0][:, 0:FT // 2, :], wb[1][:, 0:FT // 2, :], wb_raw[0]),
                  (wb[0][:, FT // 2:FT, :], wb[1][:, FT // 2:FT, :], wb_raw[1]), (wg[0][:], wg[1][:], wg_raw),
                  (bias_b[0:2, :], a_lo[0:2].rearrange("p k s -> p (k s)"), bb_raw)]
        FRONT_SPLITS, BACK_SPLITS, ALL_SPLITS = 4, 5, len(splits)

        ST = ((1, 0, 8), (0, 0, 4), (0, 4, 4), (1, 8, 8), (0, 8, 4), (0, 12, 4))
        ST_OF_GROUP = (2, 3, 5, 6)

        BANK = dict(T1=ps_a, Q=ps_c, CKV=ps_b, K=ps_c, V=ps_o, MT=ps_c, OT0=ps_b, OT1=ps_o, AT=ps_b, OP=ps_a, T2=ps_o, GT=ps_o, GX=ps_b, UP0=ps_a, UP1=ps_c, UP2=ps_a, UP3=ps_c, DN0=ps_c, DN1=ps_a, PVa=ps_o, PVb=ps_o)

        LAGS = 4

        def pipeline(eng, step):
            first, last = (LAGS + 3) // 2, (NB - 2) // 2
            for j in range(2 * first):
                step(lambda lag: Batch(j // 2, j % 2 - lag, NB))
            with eng.Fori(first, last) as i:
                for p in range(2):
                    step(lambda lag: Batch(i, p - lag, NB))
            for j in range(2 * last, NB + LAGS):
                step(lambda lag: Batch(j // 2, j % 2 - lag, NB))

        block = ctx.enter_context(nc.Block())

        @block.sync
        def _(sp):
            x_rows = x.rearrange("b (t p) d -> p (b t) d", p=P)
            out_rows = out.rearrange("b (t p) d -> p (b t) d", p=P)

            def load_x(b):
                if b.off:
                    return
                wait(sp, x_in[b.parity], 16 * b.half)
                sp.dma_start(xs[:, bass.ds(TT * b.n, TT), :], x_rows[:, bass.ds(TT * b.n, TT), :]).then_inc(x_in[b.parity], 16)

            def prefetch_x(b):
                if not (b.static and b.n < 3):
                    load_x(b)

            def store(b):
                if b.off:
                    return
                sp.wait_ge(out_ready, b.n + 1)
                sp.dma_start(out_rows[:, bass.ds(TT * b.n, TT), :], xs[:, bass.ds(TT * b.n, TT), :]).then_inc(stored[b.parity], 16)

            def load_gates(b):
                if b.off:
                    return
                wait(sp, out_ready, b.n - 1)
                sp.dma_start(gates[b.parity][:].rearrange("p g d -> p (g d)"), gates_dram[bass.ds(b.n, 1), :].to_broadcast([P, 2 * D])
                             ).then_inc(gates_in[b.parity], 16)

            def load_maxima(b):
                if b.off:
                    return
                sp.wait_ge(mt_ready, b.n + 1)
                sp.dma_start(qs[b.parity][R:RM, :, :], mx_rows[:]).then_inc(maxrows_in, 16)

            def stack(b, part, side, parts, stacks, ready, done):
                if b.off:
                    return
                wait(sp, st_done, CH * (b.n - 1))
                wait_alone(sp)
                sp.wait_ge(ready[part], b.n + 1)
                for n in range(NSPLIT):
                    if SPLITS[n][side] == part:
                        sp.dma_start(stacks[b.parity][n * HD:(n + 1) * HD, :, :], parts[:, part, :]).then_inc(done[b.parity], 16)

            def stack_q(b, part):
                stack(b, part, 0, parts_q, qs, (q1_ready, q2_ready, q3_ready), q_in)

            def stack_k(b, part):
                stack(b, part, 1, parts_k, ks, (k1_ready, k2_ready, k3_ready), k_in)

            load_x(Batch(0, 0, NB))
            sp.dma_start(cT_raw, cT.rearrange("(k p) b -> p k b", p=P)).then_inc(mod_in, 16)
            sp.dma_start(wmod_raw, wmod.rearrange("(k p) f -> p k f", p=P)).then_inc(mod_in, 16)
            for k in range(2):
                half = slice(k * C, (k + 1) * C)
                rank = slice(k * QROWS, (k + 1) * QROWS)
                sp.dma_start(wdq_raw[0:QROWS, k, :], w_dq[rank, :]).then_inc(weights_in, 16)
                sp.dma_start(wuq_raw[0:QROWS, k, :], w_uqT[rank, :]).then_inc(weights_in, 16)
                sp.dma_start(wdkv_raw[:, :, half], w_dkvT.rearrange("(k p) c -> p k c", p=P)).then_inc(weights_in, 16)
                sp.dma_start(wuk_raw[half, :], w_ukT).then_inc(weights_in, 16)
                sp.dma_start(wuv_raw[half, :], w_uvT).then_inc(weights_in, 16)
            sp.dma_start(wout_raw, w_outT.rearrange("(k p) c -> p k c", p=P)).then_inc(weights_in, 16)
            load_x(Batch(0, 1, NB))
            load_x(Batch(1, 0, NB))
            sp.dma_start(wa_raw, waT.rearrange("(k p) f -> p k f", p=P)).then_inc(ffn_in, 16)
            for k in range(2):
                half = slice(k * F // 2, (k + 1) * F // 2)
                sp.dma_start(wb_raw[k], wbT[half, :].rearrange("(k p) f -> p k f", p=P)).then_inc(ffn_in, 16)
                sp.dma_start(bb_raw[k:k + 1, :], bb).then_inc(ffn_in, 16)
            sp.dma_start(wg_raw, wgT.rearrange("(k p) f -> p k f", p=P)).then_inc(ffn_in, 16)
            sp.dma_start(bias_a[:], ba).then_inc(ffn_in, 16)
            sp.wait_ge(clamp_ready, 4)
            sp.dma_start(gates_dram, clamped).then_inc(gates_stored, 16)
            sp.wait_ge(gates_stored, 16)
            sp.wait_ge(w_lo, ALL_SPLITS)
            sp.dma_start(bias_b[1:2, :].bitcast(F32), a_lo[0:1].rearrange("p k s -> p (k s)").bitcast(F32)).then_inc(bias_lo_in, 16)

            def step(at):
                stack_q(at(0), 0)
                stack_q(at(0), 1)
                stack_k(at(0), 0)
                load_gates(at(2))
                prefetch_x(at(-1))
                stack_k(at(0), 1)
                store(at(4))
                stack_q(at(0), 2)
                load_maxima(at(1))
                stack_k(at(0), 2)

            pipeline(sp, step)
            for n in range(2):
                sp.wait_ge(stored[n], 16 * NB // 2)

        @block.tensor
        def _(pe):
            def product(outp, left, right, start, stop, **kw):
                pe.matmul(outp, left[0], right[0], start=start, stop=False, **kw)
                pe.matmul(outp, left[0], right[1], start=False, stop=False, **kw)
                return pe.matmul(outp, left[1], right[0], start=False, stop=stop, **kw)

            pe.wait_ge(mod_in, 32)
            pe.wait_ge(silu_ready, 1)
            for n, dst in enumerate((ps_s[0:NB, 0:512], ps_s[0:NB, 512:1024], ps_t[0:NB, 0:512])):
                for k in range(KT):
                    mm = pe.matmul(dst, c_silu[:, k, :], wmod_raw[:, k, n * 512:(n + 1) * 512], start=k == 0, stop=k == KT - 1)
            mm.then_inc(mod_done, 1)
            pe.wait_ge(weights_in, 16 * 11)
            for n in range(KT):
                for k in range(2):
                    mm = pe.matmul(ps_c[:, n * D:(n + 1) * D], wdq_raw[0:QROWS, k, n * P:(n + 1) * P], wuq_raw[0:QROWS, k, :],
                                   start=k == 0, stop=k == 1)
            mm.then_inc(wq_done, 1)
            pe.wait_ge(modrow_ready, 3)
            pe.wait_ge(consts_ready, 2)
            for n in range(8):
                mm = pe.transpose(ps_b[:, n * NB:(n + 1) * NB], modrow[n // 4][:, (n % 4) * P:(n % 4 + 1) * P], ident[0:NB, 0:NB])
            mm.then_inc(modt_done, 1)
            pe.wait_ge(modt_ready, 2)
            pe.wait_ge(clamp_ready, 3)
            pe.wait_ge(w_lo, FRONT_SPLITS)
            pe.wait_ge(blank, 7)
            pe.wait_ge(consts_ready, 4)

            READERS = {
                "T1": ((h32_ready, 1, 1),), "Q": ((q1_ready, 1, 1), (qr_ready, 1, 1)), "CKV": ((ckv_ready, 1, 1),),
                "K": ((k1_ready, 1, 1), (kr_ready, 1, 1)), "V": ((v_ready, 1, 1),), "MT": ((mt_ready, 1, 1),),
                "PVa": ((o_ready, 2, 1),), "PVb": ((o_ready, 2, 2),), "OT0": ((attn_ready, 2, 1),), "OT1": ((attn_ready, 2, 2),),
                "AT": ((a_hi_ready, 1, 1), (a_lo_ready, 1, 1)), "OP": ((gated_ready, 1, 1),), "T2": ((g32_ready, 1, 1),),
                "GT": ((logit_rows_ready, 1, 1),), "GX": ((logits_ready, 1, 1),),
                "UP0": ((gelu_done, 2, 1),), "UP1": ((gelu_done, 2, 2),), "UP2": ((relu_done, 2, 1),), "UP3": ((relu_done, 2, 2),),
                "DN0": ((y_ready, 2, 1),), "DN1": ((y_ready, 2, 2),)}

            def bank_left(users):
                for user, b in users:
                    if not b.off:
                        for sem, a_batch, count in READERS[user]:
                            pe.wait_ge(sem, a_batch * b.n + count)
                        return

            def s_chunk(b, c):
                if b.off:
                    return
                if c == 0:
                    pe.wait_ge(q_in[b.parity], LOADS * (b.half + 1))
                    pe.wait_ge(k_in[b.parity], LOADS * (b.half + 1))
                wait(pe, max_done, CH * b.n + c)
                tile, heads = (0, range(8 * c, 8 * c + 8)) if c < 2 else (1, range(4 * c - 8, 4 * c - 4))
                width = P * (tile + 1)
                per_bank = 512 // width
                for n, h in enumerate(heads):
                    if n % per_bank == 0:
                        bank = ps_s[:, n // per_bank * 512:(n // per_bank + 1) * 512].rearrange("p (h k) -> p h k", k=width)
                        pe.matmul(bank[:, :, width - P:width], ident_b[:], mask_b[:].unsqueeze(1).to_broadcast([P, per_bank, P]),
                                  start=True, stop=False, skip_group_check=True)
                    mm = pe.matmul(bank[:, n % per_bank, :], qs[b.parity][0:R, h, tile * P:(tile + 1) * P], ks[b.parity][0:R, h, 0:width],
                                   start=False, stop=True, skip_group_check=True)
                mm.then_inc(s_done, 1)

            def st_chunk(b, c):
                if b.off:
                    return
                if c == 0:
                    pe.wait_ge(maxrows_in, 16 * (b.n + 1))
                wait(pe, exp_done, CH * b.n + c)
                tile, h0, n = ST[c]
                width = S - P * tile
                for h in range(n):
                    mm = pe.matmul(ps_t[:, h * width:(h + 1) * width], ks[b.parity][0:RM, h0 + h, tile * P:(tile + 1) * P],
                                   qs[b.parity][0:RM, h0 + h, tile * P:S], start=True, stop=True)
                mm.then_inc(st_done, 1)

            def values(b, g, *users):
                if b.off:
                    return
                if g == 0:
                    pe.wait_ge(v_ready, b.n + 1)
                pe.wait_ge(masked, CH * b.n + ST_OF_GROUP[g])
                bank_left(users)
                for n in range(4):
                    h = 4 * g + n
                    dst = BANK["PVa"][32 * n:32 * n + HD + 1, (g % 2) * S:(g % 2 + 1) * S]
                    pe.matmul(dst, v[b.parity][:, 0, h, :], p0[:, h, :], start=True, stop=False)
                    mm = pe.matmul(dst[:, P:S], v[b.parity][:, 1, h, :], p1[:, h, :], start=False, stop=True)
                mm.then_inc(pv_done, 1)

            def turn_values(b, t, *users):
                if b.off:
                    return
                pe.wait_ge(o_ready, 2 * (b.n + 1))
                bank_left(users)
                for g in range(4):
                    mm = pe.transpose(BANK[f"OT{t}"][:, g * P:(g + 1) * P], oT[:, g, t * P:(t + 1) * P], ident[:])
                mm.then_inc(ot_done, 1)

            def turn(dst, src, done):
                for k in range(KT):
                    for t in range(TT):
                        mm = pe.transpose(dst[:, k * S + t * P:k * S + (t + 1) * P], src[:, t, k * P:(k + 1) * P], ident[:])
                mm.then_inc(done, 1)

            def turn_z1(b, *users):
                if b.off:
                    return
                pe.wait_ge(z1_ready, b.n + 1)
                bank_left(users)
                turn(BANK["T1"], z1, t1_done)

            def turn_attn(b, *users):
                if b.off:
                    return
                pe.wait_ge(attn_ready, 2 * (b.n + 1))
                bank_left(users)
                turn(BANK["AT"], attn, at_done)

            def turn_z2(b, *users):
                if b.off:
                    return
                pe.wait_ge(z2_ready, b.n + 1)
                bank_left(users)
                turn(BANK["T2"], z2, t2_done)

            def turn_maxima(b, *users):
                if b.off:
                    return
                pe.wait_ge(max_split, 4 * (b.n + 1))
                bank_left(users)
                wait_alone(pe)
                for t in range(TT):
                    mm = pe.transpose(mt_out[:, t * P:(t + 1) * P], mx_parts[:, t, :, :].rearrange("p c h -> p (c h)"), ident_b[:])
                mm.then_inc(mt_done, 1)

            def project_q(b, *users):
                if b.off:
                    return
                pe.wait_ge(h_hi_ready, b.n + 1)
                pe.wait_ge(h_lo_ready, b.n + 1)
                bank_left(users)
                for n in range(KT):
                    for k in range(KT):
                        cols = slice(n * P, (n + 1) * P)
                        mm = product(BANK["Q"][:, n * S:(n + 1) * S], (wq[0][:, k, cols], wq[1][:, k, cols]),
                                     (h_hi[:, k, :], h_lo[:, k, :]), k == 0, k == KT - 1)
                mm.then_inc(q_done, 1)

            def compress(b, *users):
                if b.off:
                    return
                pe.wait_ge(h_hi_ready, b.n + 1)
                pe.wait_ge(h_lo_ready, b.n + 1)
                bank_left(users)
                for k in range(KT):
                    mm = product(BANK["CKV"][:, 0:S], (wdkv[0][:, k, :], wdkv[1][:, k, :]), (h_hi[:, k, :], h_lo[:, k, :]),
                                 k == 0, k == KT - 1)
                mm.then_inc(ckv_done, 1)

            def expand_k(b, *users):
                if b.off:
                    return
                pe.wait_ge(ckv_ready, b.n + 1)
                bank_left(users)
                for n in range(KT):
                    for w in range(2):
                        mm = pe.matmul(BANK["K"][:, n * S:(n + 1) * S], wuk[w][:, n * P:(n + 1) * P], ckv[:], start=w == 0, stop=w == 1)
                mm.then_inc(k_done, 1)

            def expand_v(b, *users):
                if b.off:
                    return
                pe.wait_ge(ckv_ready, b.n + 1)
                bank_left(users)
                for t in range(TT):
                    for w in range(2):
                        mm = pe.matmul(BANK["V"][:, t * D:(t + 1) * D], ckv[:, t * P:(t + 1) * P], wuv[w][:], start=w == 0, stop=w == 1)
                mm.then_inc(v_done, 1)

            def project_out(b, *users):
                if b.off:
                    return
                pe.wait_ge(a_hi_ready, b.n + 1)
                pe.wait_ge(a_lo_ready, b.n + 1)
                if b.first:
                    pe.wait_ge(w_lo, BACK_SPLITS)
                bank_left(users)
                for t in range(TT):
                    tok = slice(t * P, (t + 1) * P)
                    for k in range(KT):
                        mm = product(BANK["OP"][:, t * D:(t + 1) * D], (a_hi[:, k, tok], a_lo[:, k, tok]),
                                     (wout[0][:, k, :], wout[1][:, k, :]), k == 0, k == KT - 1)
                mm.then_inc(op_done, 1)

            def gate(b, *users):
                if b.off:
                    return
                pe.wait_ge(g_hi_ready, b.n + 1)
                pe.wait_ge(g_lo_ready, b.n + 1)
                if b.first:
                    pe.wait_ge(w_lo, ALL_SPLITS)
                bank_left(users)
                for k in range(KT):
                    mm = product(BANK["GT"][0:2, 0:S], (wg[0][:, k, :], wg[1][:, k, :]), (g_hi[:, k, :], g_lo[:, k, :]), k == 0, k == KT - 1)
                mm.then_inc(gate_done, 1)

            def turn_gate(b, *users):
                if b.off:
                    return
                pe.wait_ge(logit_rows_ready, b.n + 1)
                bank_left(users)
                wait_alone(pe)
                for t in range(TT):
                    mm = pe.transpose(BANK["GX"][:, 2 * t:2 * t + 2], logit_rows[:, t * P:(t + 1) * P], ident[0:2, 0:2])
                mm.then_inc(gate_turned, 1)

            def up(b, u, *users):
                if b.off:
                    return
                pe.wait_ge(g_hi_ready, b.n + 1)
                pe.wait_ge(g_lo_ready, b.n + 1)
                if b.first:
                    pe.wait_ge(w_lo, ALL_SPLITS)
                bank_left(users)
                for n in range(2):
                    cols = slice((2 * u + n) * P, (2 * u + n + 1) * P)
                    for k in range(KT):
                        mm = product(BANK[f"UP{u}"][:, n * S:(n + 1) * S], (wa[0][:, k, cols], wa[1][:, k, cols]),
                                     (g_hi[:, k, :], g_lo[:, k, :]), k == 0, k == KT - 1)
                mm.then_inc(up_done, 1)

            def down(b, t, e, *users):
                if b.off:
                    return
                pe.wait_ge(hid_hi_ready, 4 * b.n + 2 * e + 2)
                pe.wait_ge((lo_gelu_ready, lo_relu_ready)[e], 2 * (b.n + 1))
                if b.first:
                    pe.wait_ge(bias_lo_in, 16)
                bank_left(users)
                dst = BANK[f"DN{t}"][:, e * D:(e + 1) * D]
                tok = slice(t * P, (t + 1) * P)
                pe.matmul(dst, ones_r[:], bias_b[:, e * D:(e + 1) * D], start=True, stop=False)
                for n in range(e * FT // 2, (e + 1) * FT // 2):
                    mm = product(dst, (hid_hi[:, n, tok], hid_lo[:, n, tok]), (wb[0][:, n, :], wb[1][:, n, :]),
                                 False, n == (e + 1) * FT // 2 - 1)
                mm.then_inc(dn_done, 1)

            def step(at):
                compress(at(1), ("GX", at(5)), ("AT", at(4)), ("OT0", at(4)), ("CKV", at(2)))
                st_chunk(at(3), 4)
                s_chunk(at(2), 3)
                values(at(3), 0, ("T2", at(4)), ("V", at(2)))
                st_chunk(at(3), 5)
                values(at(3), 1)
                s_chunk(at(2), 4)
                expand_k(at(1), ("Q", at(1)))
                up(at(4), 0, ("DN1", at(5)), ("T1", at(1)))
                values(at(3), 2, ("PVa", at(3)))
                s_chunk(at(2), 5)
                values(at(3), 3)
                up(at(4), 1, ("K", at(1)), ("Q", at(1)), ("DN0", at(5)))
                turn_values(at(3), 0, ("CKV", at(1)), ("GX", at(5)))
                turn_values(at(3), 1, ("PVb", at(3)))
                up(at(4), 2, ("UP0", at(4)))
                turn_maxima(at(2), ("UP1", at(4)), ("K", at(1)))
                turn_attn(at(3), ("OT0", at(3)))
                gate(at(4), ("OT1", at(3)), ("PVb", at(3)), ("PVa", at(3)), ("T2", at(4)))
                up(at(4), 3, ("MT", at(2)), ("UP1", at(4)))
                project_out(at(3), ("UP2", at(4)), ("UP0", at(4)), ("DN1", at(5)), ("T1", at(1)))
                st_chunk(at(2), 0)
                turn_gate(at(4), ("AT", at(3)), ("OT0", at(3)), ("CKV", at(1)), ("GX", at(5)))
                s_chunk(at(1), 0)
                expand_v(at(1), ("GT", at(4)), ("OT1", at(3)), ("PVb", at(3)), ("PVa", at(3)), ("T2", at(4)), ("V", at(2)))
                down(at(4), 0, 0, ("UP3", at(4)))
                turn_z1(at(0), ("OP", at(3)), ("UP2", at(4)), ("UP0", at(4)), ("DN1", at(5)), ("T1", at(1)))
                st_chunk(at(2), 1)
                down(at(4), 0, 1)
                s_chunk(at(1), 1)
                st_chunk(at(2), 2)
                down(at(4), 1, 0, ("T1", at(0)), ("OP", at(3)), ("UP2", at(4)))
                s_chunk(at(1), 2)
                st_chunk(at(2), 3)
                turn_z2(at(3), ("V", at(1)), ("GT", at(4)))
                down(at(4), 1, 1)
                project_q(at(0), ("DN0", at(4)), ("UP3", at(4)), ("MT", at(2)), ("UP1", at(4)), ("K", at(1)))

            mt_out = BANK["MT"][0:3 * NH, 0:P].bitcast(BF16)
            pipeline(pe, step)

        @block.scalar
        def _(act):
            act.wait_ge(mod_in, 32)
            act.activation(c_silu, cT_raw, ACT.Silu).then_inc(silu_ready, 1)
            for n, (hi, _, src) in enumerate(splits):
                if n == 0:
                    act.wait_ge(weights_in, 16 * 11)
                if n == 3:
                    act.wait_ge(wq_done, 1)
                if n == BACK_SPLITS:
                    act.wait_ge(ffn_in, 16 * 7)
                if n == ALL_SPLITS - 1:
                    act.wait_ge(blank, 7)
                act.activation(hi, src, ACT.Copy).then_inc(w_hi, 1)

            def values_copy(b, half):
                if b.off:
                    return
                act.wait_ge(pv_done, 4 * b.n + 2 * half + 2)
                wait(act, ot_done, 2 * b.n)
                act.activation(oT[:, 2 * half:2 * half + 2, :], BANK["PVa"][:].rearrange("p (g s) -> p g s", g=2), ACT.Copy).then_inc(o_ready, 1)

            def second_expert(b, t):
                if b.off:
                    return
                act.wait_ge(dn_done, 4 * b.n + 2 * t + 2)
                act.wait_ge(choice_ready, b.n + 1)
                wait(act, out_ready, b.n)
                act.activation(y[:, t, :], BANK[f"DN{t}"][:, D:2 * D], ACT.Copy, scale=second[b.parity][:, t:t + 1]).then_inc(second_ready, 1)

            def modulate(dst, src, base, n, ready):
                for k in range(KT):
                    ins = act.activation(dst[:, k, :], src[:, k * S:(k + 1) * S], ACT.Identity,
                                         bias=modT[:, bass.ds(n, 1), base + k], scale=modT[:, bass.ds(n, 1), base + 2 + k])
                ins.then_inc(ready, 1)

            def modulate_1(b):
                if b.off:
                    return
                act.wait_ge(t1_done, b.n + 1)
                wait(act, h_hi_ready, b.n)
                wait(act, h_lo_ready, b.n)
                modulate(h32, BANK["T1"], 0, b.n, h32_ready)

            def modulate_2(b):
                if b.off:
                    return
                act.wait_ge(t2_done, b.n + 1)
                wait(act, g_hi_ready, b.n)
                wait(act, g_lo_ready, b.n)
                modulate(g32, BANK["T2"], 4, b.n, g32_ready)

            def attn_hi(b):
                if b.off:
                    return
                act.wait_ge(at_done, b.n + 1)
                wait(act, op_done, b.n)
                act.activation(a_hi[:].rearrange("p k s -> p (k s)"), BANK["AT"][:], ACT.Copy).then_inc(a_hi_ready, 1)

            def first_part(b, src, parts, done, rest_ready, stack_in, ready):
                if b.off:
                    return
                act.wait_ge(done, b.n + 1)
                wait(act, rest_ready, b.n)
                wait(act, stack_in[1 - b.parity], LOADS * (b.half + b.parity))
                act.activation(parts[:, 0, :], src[:], ACT.Copy).then_inc(ready, 1)

            def q_first(b):
                first_part(b, BANK["Q"], parts_q, q_done, qr_ready, q_in, q1_ready)

            def k_first(b):
                first_part(b, BANK["K"], parts_k, k_done, kr_ready, k_in, k1_ready)

            def ckv_hi(b):
                if b.off:
                    return
                act.wait_ge(ckv_done, b.n + 1)
                wait(act, k_done, b.n)
                wait(act, v_done, b.n)
                act.activation(ckv[:], BANK["CKV"][:, 0:S], ACT.Copy).then_inc(ckv_hi_ready, 1)

            def v_copy(b):
                if b.off:
                    return
                act.wait_ge(v_done, b.n + 1)
                wait(act, pv_done, 4 * (b.n - 1))
                if b.static and b.n == 1:
                    act.wait_ge(blank, 8)
                act.activation(v[b.parity][:, :, :, 0:HD], BANK["V"][:].rearrange("p (t h e) -> p t h e", t=TT, h=NH), ACT.Copy).then_inc(v_ready, 1)

            def maxima_rows(b):
                if b.off:
                    return
                act.wait_ge(mt_done, b.n + 1)
                wait(act, maxrows_in, 16 * b.n)
                act.activation(mx_rows[:], BANK["MT"][0:3 * NH, 0:P].bitcast(BF16), ACT.Copy).then_inc(mt_ready, 1)

            def gelu(b, u):
                if b.off:
                    return
                act.wait_ge(up_done, 4 * b.n + u + 1)
                wait(act, hid_hi_ready, 4 * b.n - 1 + u)
                wait(act, lo_relu_ready, 2 * b.n - 1 + u)
                for n in range(2):
                    ins = act.activation(hid32[:, u, n, :], BANK[f"UP{u}"][:, n * S:(n + 1) * S], ACT.Gelu,
                                         bias=bias_a[:, 2 * u + n:2 * u + n + 1])
                ins.then_inc(gelu_done, 1)

            def exponentials(b, c):
                if b.off:
                    return
                act.wait_ge(st_done, CH * b.n + c + 1)
                wait(act, pv_done, 4 * (b.n - 1) + (2, 1, 2, 4, 3, 4)[c])
                if b.first and c == 0:
                    act.wait_ge(w_lo, ALL_SPLITS)
                tile, h0, n = ST[c]
                act.activation((p0, p1)[tile][:, h0:h0 + n, :], ps_t[:].rearrange("p (h s) -> p h s", h=n), ACT.Exp, scale=SCALE).then_inc(exp_done, 1)

            def step(at):
                exponentials(at(2), 0)
                modulate_1(at(0))
                exponentials(at(2), 1)
                v_copy(at(1))
                exponentials(at(2), 2)
                second_expert(at(4), 0)
                exponentials(at(2), 3)
                modulate_2(at(3))
                second_expert(at(4), 1)
                q_first(at(0))
                exponentials(at(2), 4)
                ckv_hi(at(0))
                exponentials(at(2), 5)
                values_copy(at(2), 0)
                k_first(at(0))
                gelu(at(3), 0)
                values_copy(at(2), 1)
                gelu(at(3), 1)
                maxima_rows(at(1))
                attn_hi(at(2))

            pipeline(act, step)

        @block.vector
        def _(dve):
            def stats(b, n):
                if b.off:
                    return
                st, mv, ve = ln_st[n], ln_mv[n], ln_ve[n]
                s_st, s_mv, s_ve, s_rs, s_z = ((st1, mv1, ve1, rs1, z1_ready), (st2, mv2, ve2, rs2, z2_ready))[n]
                if n == 0:
                    dve.wait_ge(x_in[b.parity], 16 * (b.half + 1))
                else:
                    dve.wait_ge(x1_ready, b.n + 1)
                wait(dve, s_mv, TT * b.n)
                wait(dve, s_rs, b.n)
                wait(dve, s_z, b.n)
                for t in range(TT):
                    dve.bn_stats(st[:, t, :], xs[:, bass.ds(TT * b.n + t, 1), :].rearrange("p a d -> p (a d)")).then_inc(s_st, 1)
                for t in range(TT):
                    dve.wait_ge(s_st, TT * b.n + t + 1)
                    wait_alone(dve)
                    dve.bn_aggr(mv[:, t, :], st[:, t, :]).then_inc(s_mv, 1)
                dve.wait_ge(s_mv, TT * (b.n + 1))
                dve.tensor_scalar(ve[:], mv[:, :, 1], EPS, None, ALU.add).then_inc(s_ve, 1)

            def normalise(b, n):
                if b.off:
                    return
                dst, ready, s_rs, turned = ((z1, z1_ready, rs1, t1_done), (z2, z2_ready, rs2, t2_done))[n]
                dve.wait_ge(s_rs, b.n + 1)
                wait(dve, turned, b.n)
                for t in range(TT):
                    ins = dve.tensor_scalar(dst[:, t, :], xs[:, bass.ds(TT * b.n + t, 1), :].rearrange("p a d -> p (a d)"),
                                            ln_mv[n][:, t, 0:1], ln_rs[n][:, t:t + 1], ALU.subtract, ALU.mult)
                ins.then_inc(ready, 1)

            dve.memset(neg_half[:], -0.5).then_inc(blank, 1)
            dve.memset(bias_b[:].bitcast(F32), 0.0).then_inc(blank, 1)
            dve.memset(ones_r[:].bitcast(F32), 1.0).then_inc(blank, 1)
            dve.memset(v[0][:, :, :, HD:HD + 1], 1.0).then_inc(blank, 1)
            dve.memset(ps_o[:], 0.0).then_inc(blank, 1)
            for n in range(2):
                dve.memset(ks[n][R:RM, :, :], 1.0).then_inc(blank, 1)
            dve.wait_ge(mod_done, 1)
            dve.tensor_copy(modrow[0], ps_s[0:NB, 0:2 * D]).then_inc(modrow_ready, 1)
            dve.tensor_copy(modrow[1][:, 0:D], ps_s[0:NB, 3 * D:4 * D]).then_inc(modrow_ready, 1)
            dve.tensor_copy(modrow[1][:, D:2 * D], ps_t[0:NB, 0:D]).then_inc(modrow_ready, 1)
            gate_rows = (ps_s[0:NB, 2 * D:3 * D], ps_t[0:NB, D:2 * D])
            for n, src in enumerate(gate_rows):
                half = slice(n * D, (n + 1) * D)
                ins = dve.tensor_scalar(sign[:, half], src, 0.0, 2.0, ALU.is_ge, ALU.mult)
            ins.then_inc(clamp_ready, 1)
            dve.wait_ge(clamp_ready, 1)
            dve.tensor_scalar(sign, sign, -1.0, None, ALU.add).then_inc(clamp_ready, 1)
            dve.wait_ge(clamp_ready, 2)
            for n, src in enumerate(gate_rows):
                half = slice(n * D, (n + 1) * D)
                ins = dve.tensor_tensor(clamped[:, half], src, sign[:, half], ALU.mult)
            ins.then_inc(clamp_ready, 1)
            dve.wait_ge(clamp_ready, 3)
            dve.scalar_tensor_tensor(out=clamped, in0=clamped, scalar=LEAST_GATE, in1=sign, op0=ALU.max, op1=ALU.mult).then_inc(clamp_ready, 1)
            dve.wait_ge(modt_done, 1)
            turned = ps_b[:, 0:8 * NB].rearrange("p (u w k b) -> p u w k b", u=2, w=2, k=KT)
            by_batch = modT[:].rearrange("p b (u w k) -> p u w k b", u=2, w=2)
            for w in range(2):
                for u in range(2):
                    ins = dve.tensor_scalar(by_batch[:, u, w], turned[:, u, w], float(w), None, ALU.add)
                ins.then_inc(modt_ready, 1)
            for n, (hi, lo, src) in enumerate(splits):
                dve.wait_ge(w_hi, n + 1)
                dve.tensor_tensor(lo, src, hi.bitcast(F32), ALU.subtract).then_inc(w_lo, 1)
            dve.wait_ge(w_lo, ALL_SPLITS)
            dve.memset(v[1][:, :, :, HD:HD + 1], 1.0).then_inc(blank, 1)

            def row_max(b, c):
                if b.off:
                    return
                dve.wait_ge(s_done, CH * b.n + c + 1)
                if c == 0:
                    wait(dve, max_split, 4 * b.n)
                if c < 2:
                    dst, n = mx[:, 0, 8 * c:8 * c + 8], 8
                else:
                    dst, n = mx[:, 1, 4 * c - 8:4 * c - 4], 4
                dve.tensor_reduce(dst, ps_s[:].rearrange("p (h k) -> p h k", h=n), AX_X, ALU.max).then_inc(max_done, 1)

            def split_maxima(b):
                if b.off:
                    return
                dve.wait_ge(max_done, CH * (b.n + 1))
                wait(dve, mt_done, b.n)
                dve.tensor_scalar(mx_parts[:, :, 0, :], mx[:], -1.0, None, ALU.mult).then_inc(max_split, 1)
                dve.wait_ge(max_split, 4 * b.n + 1)
                dve.scalar_tensor_tensor(out=mx_rest[:], in0=mx[:], scalar=-1.0, in1=mx_parts[:, :, 0, :],
                                         op0=ALU.mult, op1=ALU.subtract).then_inc(max_split, 1)
                dve.wait_ge(max_split, 4 * b.n + 2)
                dve.tensor_copy(mx_parts[:, :, 1, :], mx_rest[:]).then_inc(max_split, 1)
                dve.wait_ge(max_split, 4 * b.n + 3)
                dve.tensor_tensor(mx_parts[:, :, 2, :], mx_rest[:], mx_parts[:, :, 1, :], ALU.subtract).then_inc(max_split, 1)

            def divide(b, t):
                if b.off:
                    return
                src = BANK[f"OT{t}"][:].rearrange("p (h e) -> p h e", h=NH)
                dve.wait_ge(ot_done, 2 * b.n + t + 1)
                dve.reciprocal(rden[:, t, :], src[:, :, HD]).then_inc(rden_ready, 1)
                dve.wait_ge(rden_ready, 2 * b.n + t + 1)
                wait(dve, at_done, b.n)
                dve.tensor_tensor(attn[:, t, :].rearrange("p (h e) -> p h e", h=NH), src[:, :, 0:HD],
                                  rden[:, t, :].unsqueeze(2).to_broadcast([P, NH, HD]), ALU.mult).then_inc(attn_ready, 1)

            def add_first_expert(b, t):
                if b.off:
                    return
                dve.wait_ge(second_ready, 2 * b.n + t + 1)
                dve.scalar_tensor_tensor(out=y[:, t, :], in0=BANK[f"DN{t}"][:, 0:D], scalar=first[b.parity][:, t:t + 1], in1=y[:, t, :],
                                         op0=ALU.mult, op1=ALU.add).then_inc(y_ready, 1)

            def part_rest(b, src, parts, rest, done, first_ready_, rest_ready, third_ready):
                if b.off:
                    return
                dve.wait_ge(done, b.n + 1)
                dve.wait_ge(first_ready_, b.n + 1)
                wait(dve, third_ready, b.n)
                dve.tensor_tensor(rest[:], src[:], parts[:, 0, :], ALU.subtract).then_inc(rest_ready, 1)

            def second_part(b, parts, rest, rest_ready, ready):
                if b.off:
                    return
                dve.wait_ge(rest_ready, b.n + 1)
                dve.tensor_copy(parts[:, 1, :], rest[:]).then_inc(ready, 1)

            def q_rest(b):
                part_rest(b, BANK["Q"], parts_q, rest_q, q_done, q1_ready, qr_ready, q3_ready)

            def k_rest(b):
                part_rest(b, BANK["K"], parts_k, rest_k, k_done, k1_ready, kr_ready, k3_ready)

            def q_second(b):
                second_part(b, parts_q, rest_q, qr_ready, q2_ready)

            def k_second(b):
                second_part(b, parts_k, rest_k, kr_ready, k2_ready)

            def attn_low(b):
                if b.off:
                    return
                dve.wait_ge(a_hi_ready, b.n + 1)
                wait(dve, op_done, b.n)
                dve.tensor_tensor(a_lo[:].rearrange("p k s -> p (k s)"), BANK["AT"][:], a_hi[:].rearrange("p k s -> p (k s)").bitcast(F32),
                                  ALU.subtract).then_inc(a_lo_ready, 1)

            def gate_attn(b):
                if b.off:
                    return
                dve.wait_ge(op_done, b.n + 1)
                dve.wait_ge(gates_in[b.parity], 16 * (b.half + 1))
                wait(dve, x1_ready, b.n)
                for t in range(TT):
                    ins = dve.tensor_tensor(gated[:, t, :], BANK["OP"][:, t * D:(t + 1) * D], gates[b.parity][:, 0, :], ALU.mult)
                ins.then_inc(gated_ready, 1)

            def h_high(b):
                if b.off:
                    return
                dve.wait_ge(h32_ready, b.n + 1)
                wait(dve, q_done, b.n)
                wait(dve, ckv_done, b.n)
                dve.tensor_copy(h_hi[:], h32[:]).then_inc(h_hi_ready, 1)

            def ckv_low(b):
                if b.off:
                    return
                dve.wait_ge(ckv_hi_ready, b.n + 1)
                dve.tensor_tensor(ckv[C:2 * C, :], BANK["CKV"][C:2 * C, 0:S], ckv[C:2 * C, :].bitcast(F32), ALU.subtract).then_inc(ckv_ready, 1)

            def g_high(b):
                if b.off:
                    return
                dve.wait_ge(g32_ready, b.n + 1)
                wait(dve, up_done, 4 * b.n)
                wait(dve, gate_done, b.n)
                dve.tensor_copy(g_hi[:], g32[:]).then_inc(g_hi_ready, 1)

            def gate_copy(b):
                if b.off:
                    return
                dve.wait_ge(gate_done, b.n + 1)
                wait(dve, gate_turned, b.n)
                dve.tensor_copy(logit_rows[:], BANK["GT"][0:2, 0:S]).then_inc(logit_rows_ready, 1)

            def choose_expert(b):
                if b.off:
                    return
                dve.wait_ge(gate_turned, b.n + 1)
                wait(dve, y_ready, 2 * (b.n - 1))
                wait(dve, choice_ready, b.n)
                dve.tensor_copy(logits[:], BANK["GX"][:, 0:2 * TT].rearrange("p (t e) -> p t e", e=2)).then_inc(logits_ready, 1)
                dve.wait_ge(logits_ready, b.n + 1)
                dve.tensor_tensor(first[b.parity][:], logits[:, :, 0], logits[:, :, 1], ALU.is_ge).then_inc(first_ready, 1)
                dve.wait_ge(first_ready, b.n + 1)
                dve.tensor_scalar(second[b.parity][:], first[b.parity][:], -1.0, 1.0, ALU.mult, ALU.add).then_inc(choice_ready, 1)

            def relu(b, u):
                if b.off:
                    return
                dve.wait_ge(up_done, 4 * b.n + u + 1)
                dve.wait_ge(lo_gelu_ready, 2 * b.n + u - 1)
                dve.wait_ge(hid_hi_ready, 4 * b.n + u - 1)
                for n in range(2):
                    ins = dve.tensor_scalar(hid32[:, u - 2, n, :], BANK[f"UP{u}"][:, n * S:(n + 1) * S],
                                            bias_a[:, 2 * u + n:2 * u + n + 1], 0.0, ALU.add, ALU.max)
                ins.then_inc(relu_done, 1)

            def hidden_high(b, u):
                if b.off:
                    return
                if u < 2:
                    dve.wait_ge(gelu_done, 2 * b.n + u + 1)
                else:
                    dve.wait_ge(relu_done, 2 * b.n + u - 1)
                wait(dve, dn_done, 4 * b.n)
                dve.tensor_copy(hid_hi[:, 2 * u:2 * u + 2, :], hid32[:, u % 2, :, :]).then_inc(hid_hi_ready, 1)

            def hidden_low(b, u):
                if b.off:
                    return
                dve.wait_ge(hid_hi_ready, 4 * b.n + u + 1)
                dve.tensor_tensor(hid_lo[:, 2 * u:2 * u + 2, :], hid32[:, u - 2, :, :],
                                  hid_hi[:, 2 * u:2 * u + 2, :].bitcast(F32), ALU.subtract).then_inc(lo_relu_ready, 1)

            def step(at):
                k_rest(at(1))
                k_second(at(1))
                row_max(at(2), 5)
                hidden_high(at(4), 0)
                split_maxima(at(2))
                divide(at(3), 0)
                divide(at(3), 1)
                hidden_high(at(4), 1)
                relu(at(4), 2)
                hidden_high(at(4), 2)
                attn_low(at(3))
                stats(at(0), 0)
                gate_copy(at(4))
                relu(at(4), 3)
                gate_attn(at(3))
                hidden_low(at(4), 2)
                normalise(at(0), 0)
                hidden_high(at(4), 3)
                hidden_low(at(4), 3)
                row_max(at(1), 0)
                stats(at(3), 1)
                h_high(at(0))
                row_max(at(1), 1)
                choose_expert(at(4))
                normalise(at(3), 1)
                add_first_expert(at(4), 0)
                row_max(at(1), 2)
                q_rest(at(0))
                g_high(at(3))
                row_max(at(1), 3)
                add_first_expert(at(4), 1)
                ckv_low(at(0))
                q_second(at(0))
                row_max(at(1), 4)

            pipeline(dve, step)

        @block.gpsimd
        def _(pool):
            pool.memset(ident[:], 0.0).then_inc(consts_ready, 1)
            pool.wait_ge(consts_ready, 1)
            pool.affine_select(out=ident[:], in_=ident[:], compare_op=ALU.not_equal, fill=1.0, base=0,
                               pattern=[[-1, P]], channel_multiplier=1).then_inc(consts_ready, 1)
            pool.wait_ge(consts_ready, 2)
            pool.tensor_copy(ident_b[:], ident[:]).then_inc(consts_ready, 1)
            pool.memset(mask_b[:], 0.0).then_inc(mask_blank, 1)
            pool.wait_ge(mask_blank, 1)
            pool.affine_select(out=mask_b[:], in_=mask_b[:], compare_op=ALU.is_ge, fill=NEG, base=0,
                               pattern=[[-1, P]], channel_multiplier=1).then_inc(consts_ready, 1)

            def inverse_deviation(b, n):
                if b.off:
                    return
                ve, rs = ln_ve[n], ln_rs[n]
                s_ve, s_rs, used = ((ve1, rs1, z1_ready), (ve2, rs2, z2_ready))[n]
                pool.wait_ge(s_ve, b.n + 1)
                wait(pool, used, b.n)
                pool.tensor_tensor(rs[:], ve[:], neg_half[:], ALU.pow).then_inc(s_rs, 1)

            def add_attn(b):
                if b.off:
                    return
                pool.wait_ge(gated_ready, b.n + 1)
                wait_alone(pool)
                rows = xs[:, bass.ds(TT * b.n, TT), :]
                pool.tensor_tensor(rows, gated[:], rows, ALU.add).then_inc(x1_ready, 1)

            def gate_ffn(b):
                if b.off:
                    return
                pool.wait_ge(y_ready, 2 * (b.n + 1))
                for t in range(TT):
                    ins = pool.tensor_tensor(y[:, t, :], y[:, t, :], gates[b.parity][:, 1, :], ALU.mult)
                ins.then_inc(scaled, 1)

            def add_ffn(b):
                if b.off:
                    return
                pool.wait_ge(scaled, b.n + 1)
                wait_alone(pool)
                rows = xs[:, bass.ds(TT * b.n, TT), :]
                pool.tensor_tensor(rows, y[:], rows, ALU.add).then_inc(out_ready, 1)

            def h_low(b):
                if b.off:
                    return
                pool.wait_ge(h_hi_ready, b.n + 1)
                pool.tensor_tensor(h_lo[:], h32[:], h_hi[:].bitcast(F32), ALU.subtract).then_inc(h_lo_ready, 1)

            def g_low(b):
                if b.off:
                    return
                pool.wait_ge(g_hi_ready, b.n + 1)
                pool.tensor_tensor(g_lo[:], g32[:], g_hi[:].bitcast(F32), ALU.subtract).then_inc(g_lo_ready, 1)

            def q_third(b):
                if b.off:
                    return
                pool.wait_ge(q2_ready, b.n + 1)
                pool.tensor_tensor(parts_q[:, 2, :], rest_q[:], parts_q[:, 1, :], ALU.subtract).then_inc(q3_ready, 1)

            def k_third(b):
                if b.off:
                    return
                pool.wait_ge(k2_ready, b.n + 1)
                pool.tensor_tensor(parts_k[:, 2, :], rest_k[:], parts_k[:, 1, :], ALU.subtract).then_inc(k3_ready, 1)

            def hidden_low(b, u):
                if b.off:
                    return
                pool.wait_ge(hid_hi_ready, 4 * b.n + u + 1)
                pool.tensor_tensor(hid_lo[:, 2 * u:2 * u + 2, :], hid32[:, u, :, :],
                                   hid_hi[:, 2 * u:2 * u + 2, :].bitcast(F32), ALU.subtract).then_inc(lo_gelu_ready, 1)

            def hide(b, c):
                if b.off:
                    return
                tile, h0, n = ST[c]
                pool.wait_ge(exp_done, CH * b.n + c + 1)
                wait_alone(pool)
                diag = (p0, p1)[tile][:, h0:h0 + n, 0:P]
                pool.affine_select(out=diag, in_=diag, compare_op=ALU.is_ge, fill=0.0, base=0,
                                   pattern=[[0, n], [1, P]], channel_multiplier=-1).then_inc(masked, 1)

            pool.wait_ge(blank, 1)

            def step(at):
                q_third(at(1))
                k_third(at(1))
                hidden_low(at(4), 0)
                hidden_low(at(4), 1)
                inverse_deviation(at(0), 0)
                add_attn(at(3))
                inverse_deviation(at(3), 1)
                h_low(at(0))
                hide(at(2), 0)
                hide(at(2), 1)
                hide(at(2), 2)
                hide(at(2), 3)
                g_low(at(3))
                hide(at(2), 4)
                hide(at(2), 5)
                gate_ffn(at(4))
                add_ffn(at(4))

            pipeline(pool, step)


def kernel(L0_attn_x, L0_attn_w_dq, L0_attn_w_uq, L0_attn_w_dkv, L0_attn_w_ukv, L0_attn_w_out, L0_ffn_Wg,
           L0_ffn_W0a, L0_ffn_b0a, L0_ffn_W0b, L0_ffn_b0b, L0_ffn_W1a, L0_ffn_b1a, L0_ffn_W1b, L0_ffn_b1b, L0_c, L0_wmod):
    import numpy as np
    import concourse.bacc as bacc
    from concourse.bass_utils import run_bass_kernel_spmd

    n = np.ascontiguousarray
    nh, hd = 16, 16
    w_uk, w_uv = np.split(np.asarray(L0_attn_w_ukv), 2, axis=0)

    def by_tile(w):
        return n(np.asarray(w).T.reshape(-1, nh // 2, 2, hd).transpose(0, 2, 3, 1).reshape(w.shape[1], nh * hd))

    arrays = {
        "x": n(L0_attn_x), "w_dq": n(L0_attn_w_dq), "w_uqT": by_tile(L0_attn_w_uq), "w_dkvT": n(np.asarray(L0_attn_w_dkv).T),
        "w_ukT": by_tile(w_uk), "w_uvT": n(w_uv.T), "w_outT": n(np.asarray(L0_attn_w_out).T), "wgT": n(np.asarray(L0_ffn_Wg).T),
        "waT": n(np.concatenate([np.asarray(L0_ffn_W0a), np.asarray(L0_ffn_W1a)], axis=0).T),
        "wbT": n(np.concatenate([np.asarray(L0_ffn_W0b), np.asarray(L0_ffn_W1b)], axis=1).T),
        "ba": n(np.concatenate([np.asarray(L0_ffn_b0a), np.asarray(L0_ffn_b1a)]).reshape(-1, P).T),
        "bb": n(np.concatenate([np.asarray(L0_ffn_b0b), np.asarray(L0_ffn_b1b)])[None, :]),
        "cT": n(np.asarray(L0_c).T), "wmod": n(L0_wmod),
    }
    nc = bacc.Bacc("TRN2", target_bir_lowering=False, num_devices=1, dynamic_dma_scratch_size=8192)
    aps = {k: nc.dram_tensor(k, a.shape, F32, kind="ExternalInput").ap() for k, a in arrays.items()}
    out = nc.dram_tensor("out", arrays["x"].shape, F32, kind="ExternalOutput").ap()
    block_kernel(nc, **aps, out=out)
    result = run_bass_kernel_spmd(nc, [arrays], core_ids=[0])
    return result.results[0]["out"]
```

```python
from contextlib import ExitStack

import concourse.bass as bass
from concourse import mybir

ALU = mybir.AluOpType
ACT = mybir.ActivationFunctionType
AX_X = mybir.AxisListType.X
F32 = mybir.dt.float32
F32R = mybir.dt.float32r
BF16 = mybir.dt.bfloat16

P = 128
EPS = 1e-5
NEG = -3.0e38
LEAST_GATE = 0.25
SPLITS = ((0, 0), (0, 1), (0, 2), (1, 0), (1, 1), (2, 0))


def wait(eng, sem, value):
    if not isinstance(value, int) or value > 0:
        eng.wait_ge(sem, value)


class Batch:

    def __init__(self, i, k, batches):
        self.n, self.half, self.parity = 2 * i + k, i + k // 2, k % 2
        self.static = isinstance(i, int)
        self.off = self.static and not 0 <= self.n < batches
        self.first = self.static and self.n == 0


def wait_alone(eng):
    eng.nop(nofuse=True)


def block_kernel(nc, x, w_dq, w_uqT, w_dkvT, w_ukT, w_uvT, w_outT, wgT, waT, wbT, ba, bb, cT, wmod, out):
    NB, S, D = x.shape
    QC = w_dq.shape[0]
    C = w_dkvT.shape[1]
    HD = 16
    NH = D // HD
    KT = D // P
    TT = S // P
    F = waT.shape[1]
    FT = F // P
    SCALE = float(HD) ** -0.5
    QROWS = QC // 2
    NSPLIT = len(SPLITS)
    R = NSPLIT * HD
    RM = R + 3
    G8 = P // HD
    assert S == 2 * P and D == 2 * P and C == 64 and NH == 16 and F == 4 * D and NB % 2 == 0 and NB >= 8
    CH = 6
    LOADS = 16 * NSPLIT

    ctx = ExitStack()

    def sb(name, shape, dt=F32):
        return ctx.enter_context(nc.sbuf_tensor(name, shape, dt))

    def psum(name):
        return ctx.enter_context(nc.psum_tensor(name, [P, 512], F32))

    def sem(name):
        return ctx.enter_context(nc.semaphore(name))

    with ctx:
        ps_s = ctx.enter_context(nc.psum_tensor("ps_s", [P, 1024], F32))
        ps_t = ctx.enter_context(nc.psum_tensor("ps_t", [P, 1024], F32))
        ps_o = psum("ps_o")
        ps_a, ps_b, ps_c = psum("ps_a"), psum("ps_b"), psum("ps_c")

        xs = sb("xs", [P, NB * TT, D])
        wq = [sb(f"wq{i}", [P, KT, D], F32R) for i in range(2)]
        wdkv = [sb(f"wdkv{i}", [P, KT, 2 * C], F32R) for i in range(2)]
        wuk = [sb(f"wuk{i}", [P, D], F32R) for i in range(2)]
        wuv = [sb(f"wuv{i}", [P, D], F32R) for i in range(2)]
        wout = [sb(f"wout{i}", [P, KT, D], F32R) for i in range(2)]
        wg = [sb(f"wg{i}", [P, KT, 2], F32R) for i in range(2)]
        wa = [sb(f"wa{i}", [P, KT, F], F32R) for i in range(2)]
        wb = [sb(f"wb{i}", [P, FT, D], F32R) for i in range(2)]
        bias_a = sb("bias_a", [P, FT])
        bias_b = sb("bias_b", [P, 2 * D])
        ident = sb("ident", [P, P])
        ident_b = sb("ident_b", [P, P], BF16)
        neg_half = sb("neg_half", [P, TT])
        modT = sb("modT", [P, NB, 8])
        z1 = sb("z1", [P, TT, D])
        h32 = sb("h32", [P, KT, S])
        h_hi, h_lo = sb("h_hi", [P, KT, S], F32R), sb("h_lo", [P, KT, S], F32R)
        parts_q, parts_k = sb("parts_q", [P, 3, KT * S], BF16), sb("parts_k", [P, 3, KT * S], BF16)
        rest_q, rest_k = sb("rest_q", [P, KT * S]), sb("rest_k", [P, KT * S])
        ckv = sb("ckv", [P, S], F32R)
        v = [sb(f"v{i}", [P, TT, NH, HD + 1]) for i in range(2)]
        qs = [sb(f"qs{i}", [RM, NH, S], BF16) for i in range(2)]
        ks = [sb(f"ks{i}", [RM, NH, S], BF16) for i in range(2)]
        score_rows = [sb(f"score_rows{i}", [P, 1024]) for i in range(2)]
        mx = sb("mx", [P, TT, NH])
        mx_parts = sb("mx_parts", [P, TT, 3, NH], BF16)
        mx_rest = sb("mx_rest", [P, TT, NH])
        mx_rows = sb("mx_rows", [3 * NH, S], BF16)
        p0 = sb("p0", [P, NH, S])
        p1 = sb("p1", [P, NH, P])
        oT = sb("oT", [P, 4, S])
        rden = sb("rden", [P, TT, NH])
        attn = sb("attn", [P, TT, D])
        a_hi, a_lo = sb("a_hi", [P, KT, S], F32R), sb("a_lo", [P, KT, S], F32R)
        z2 = sb("z2", [P, TT, D])
        gated = z2
        g32 = sb("g32", [P, KT, S])
        g_hi, g_lo = sb("g_hi", [P, KT, S], F32R), sb("g_lo", [P, KT, S], F32R)
        logit_rows = sb("logit_rows", [2, S])
        logits = sb("logits", [P, TT, 2])
        first = [sb(f"first{i}", [P, TT]) for i in range(2)]
        second = [sb(f"second{i}", [P, TT]) for i in range(2)]
        hid32 = sb("hid32", [P, 2, 2, S])
        hid_hi, hid_lo = sb("hid_hi", [P, FT, S], F32R), sb("hid_lo", [P, FT, S], F32R)
        y = sb("y", [P, TT, D])
        gates = [sb(f"gates{i}", [P, 2, D]) for i in range(2)]
        ln_st = [sb(f"ln_st{i}", [P, TT, 6]) for i in range(2)]
        ln_mv = [sb(f"ln_mv{i}", [P, TT, 2]) for i in range(2)]
        ln_ve = [sb(f"ln_ve{i}", [P, TT]) for i in range(2)]
        ln_rs = [sb(f"ln_rs{i}", [P, TT]) for i in range(2)]
        gates_dram = nc.dram_tensor("gates_scratch", (NB, 2 * D), F32, kind="Internal").ap()

        raw = p0[:].rearrange("p h s -> p (h s)")
        cuts = [KT * 6 * D, KT * D, KT * 2 * C, D]
        at = [sum(cuts[:i]) for i in range(5)]
        wmod_raw = raw[:, at[0]:at[1]].rearrange("p (k f) -> p k f", k=KT)
        wout_raw = raw[:, at[1]:at[2]].rearrange("p (k f) -> p k f", k=KT)
        wdkv_raw = raw[:, at[2]:at[3]].rearrange("p (k f) -> p k f", k=KT)
        wuk_raw = raw[:, at[3]:at[4]]
        wa_raw = p1[:].rearrange("p h s -> p (h s)").rearrange("p (k f) -> p k f", k=KT)
        wb_raw = [hid32[:].rearrange("p a b s -> p (a b) s"), oT[:]]
        wdq_raw, wuq_raw, wuv_raw, wg_raw = z2[:], attn[:], score_rows[0][:, 0:D], logits[:]
        cT_raw, c_silu = mx[:], mx_rest[:]
        clamped, sign = [g[:].rearrange("p g d -> p (g d)")[0:NB] for g in gates]

        x_in0, x_in1, weights_in, mod_in, mod_rest_in = (sem(n) for n in
            "x_in0 x_in1 weights_in mod_in mod_rest_in".split())
        ffn_in, silu_ready, mod_done, clamp_ready, gates_stored, modt_ready = (sem(n) for n in
            "ffn_in silu_ready mod_done clamp_ready gates_stored modt_ready".split())
        wq_done, w_hi, w_lo, blank, ones_ready, consts_ready = (sem(n) for n in
            "wq_done w_hi w_lo blank ones_ready consts_ready".split())
        gates_in0, gates_in1, stored0, stored1, q_in0, q_in1, k_in0, k_in1, maxrows_in = (sem(n) for n in
            "gates_in0 gates_in1 stored0 stored1 q_in0 q_in1 k_in0 k_in1 maxrows_in".split())
        z1_ready, t1_done, h32_ready, h_hi_ready, h_lo_ready = (sem(n) for n in
            "z1_ready t1_done h32_ready h_hi_ready h_lo_ready".split())
        q_done, q1_ready, qr_ready, q2_ready, q3_ready, k_done, k1_ready, kr_ready, k2_ready, k3_ready = (sem(n) for n in
            "q_done q1_ready qr_ready q2_ready q3_ready k_done k1_ready kr_ready k2_ready k3_ready".split())
        ckv_done, ckv_hi_ready, ckv_ready, v_done, v_ready = (sem(n) for n in
            "ckv_done ckv_hi_ready ckv_ready v_done v_ready".split())
        s_done, scores_out, scores_hidden, max_done, max_split, mt_done = (sem(n) for n in
            "s_done scores_out scores_hidden max_done max_split mt_done".split())
        mt_ready, st_done, exp_done, masked, pv_done, o_ready = (sem(n) for n in
            "mt_ready st_done exp_done masked pv_done o_ready".split())
        ot_done, rden_ready, attn_ready, at_done, a_hi_ready, a_lo_ready, op_done, gated_ready, x1_ready = (sem(n) for n in
            "ot_done rden_ready attn_ready at_done a_hi_ready a_lo_ready op_done gated_ready x1_ready".split())
        z2_ready, t2_done, g32_ready, g_hi_ready, g_lo_ready = (sem(n) for n in
            "z2_ready t2_done g32_ready g_hi_ready g_lo_ready".split())
        gate_done, logit_rows_ready, gate_turned, logits_ready, first_ready, choice_ready = (sem(n) for n in
            "gate_done logit_rows_ready gate_turned logits_ready first_ready choice_ready".split())
        up_done, gelu_done, relu_done, hid_hi_ready, lo_gelu_ready, lo_relu_ready = (sem(n) for n in
            "up_done gelu_done relu_done hid_hi_ready lo_gelu_ready lo_relu_ready".split())
        dn_done, second_ready, picked, biased, y_ready, scaled, out_ready = (sem(n) for n in
            "dn_done second_ready picked biased y_ready scaled out_ready".split())
        st1, mv1, ve1, rs1, st2, mv2, ve2, rs2 = (sem(n) for n in
            "st1 mv1 ve1 rs1 st2 mv2 ve2 rs2".split())
        x_in, gates_in, stored = (x_in0, x_in1), (gates_in0, gates_in1), (stored0, stored1)
        q_in, k_in = (q_in0, q_in1), (k_in0, k_in1)

        splits = [(wdkv[0][:], wdkv[1][:], wdkv_raw), (wuk[0][:], wuk[1][:], wuk_raw), (wuv[0][:], wuv[1][:], wuv_raw),
                  (wq[0][:], wq[1][:], ps_c[:].rearrange("p (k f) -> p k f", k=KT)), (wout[0][:], wout[1][:], wout_raw),
                  (wa[0][:], wa[1][:], wa_raw), (wb[0][:, 0:FT // 2, :], wb[1][:, 0:FT // 2, :], wb_raw[0]),
                  (wb[0][:, FT // 2:FT, :], wb[1][:, FT // 2:FT, :], wb_raw[1]), (wg[0][:], wg[1][:], wg_raw)]
        FRONT_SPLITS, BACK_SPLITS, ALL_SPLITS = 4, 5, len(splits)

        ST = ((1, 0, 8), (0, 0, 4), (0, 4, 4), (1, 8, 8), (0, 8, 4), (0, 12, 4))
        ST_OF_GROUP = (2, 3, 5, 6)

        BANK = dict(T1=ps_a, Q=ps_c, CKV=ps_b, K=ps_b, V=ps_o, MT=ps_c, OT0=ps_o, OT1=ps_b, AT=ps_b, OP=ps_c, T2=ps_c,
                    GT=ps_a, GX=ps_b, UP0=ps_c, UP1=ps_a, UP2=ps_c, UP3=ps_o, DN0=ps_o, DN1=ps_a, PVa=ps_o, PVb=ps_o)

        LAGS = 4

        def pipeline(eng, step):
            first, last = (LAGS + 3) // 2, (NB - 2) // 2
            for j in range(2 * first):
                step(lambda lag: Batch(j // 2, j % 2 - lag, NB))
            with eng.Fori(first, last) as i:
                for p in range(2):
                    step(lambda lag: Batch(i, p - lag, NB))
            for j in range(2 * last, NB + LAGS):
                step(lambda lag: Batch(j // 2, j % 2 - lag, NB))

        block = ctx.enter_context(nc.Block())

        @block.sync
        def _(sp):
            x_rows = x.rearrange("b (t p) d -> p (b t) d", p=P)
            out_rows = out.rearrange("b (t p) d -> p (b t) d", p=P)

            def load_x(b):
                if b.off:
                    return
                wait(sp, x_in[b.parity], 16 * b.half)
                sp.dma_start(xs[:, bass.ds(TT * b.n, TT), :], x_rows[:, bass.ds(TT * b.n, TT), :]).then_inc(x_in[b.parity], 16)

            def prefetch_x(b):
                if not (b.static and b.n < 3):
                    load_x(b)

            def store(b):
                if b.off:
                    return
                sp.wait_ge(out_ready, b.n + 1)
                sp.dma_start(out_rows[:, bass.ds(TT * b.n, TT), :], xs[:, bass.ds(TT * b.n, TT), :]).then_inc(stored[b.parity], 16)

            def load_gates(b):
                if b.off:
                    return
                if b.first:
                    sp.wait_ge(clamp_ready, 4)
                    sp.dma_start(gates_dram, clamped).then_inc(gates_stored, 16)
                    sp.wait_ge(gates_stored, 16)
                wait(sp, out_ready, b.n - 1)
                sp.dma_start(gates[b.parity][:].rearrange("p g d -> p (g d)"), gates_dram[bass.ds(b.n, 1), :].to_broadcast([P, 2 * D])
                             ).then_inc(gates_in[b.parity], 16)

            def load_maxima(b):
                if b.off:
                    return
                sp.wait_ge(mt_ready, b.n + 1)
                sp.dma_start(qs[b.parity][R:RM, :, :], mx_rows[:]).then_inc(maxrows_in, 16)

            def stack(b, part, side, parts, stacks, ready, done):
                if b.off:
                    return
                wait(sp, st_done, CH * (b.n - 1))
                wait_alone(sp)
                sp.wait_ge(ready[part], b.n + 1)
                for n in range(NSPLIT):
                    if SPLITS[n][side] == part:
                        sp.dma_start(stacks[b.parity][n * HD:(n + 1) * HD, :, :], parts[:, part, :]).then_inc(done[b.parity], 16)

            def stack_q(b, part):
                stack(b, part, 0, parts_q, qs, (q1_ready, q2_ready, q3_ready), q_in)

            def stack_k(b, part):
                stack(b, part, 1, parts_k, ks, (k1_ready, k2_ready, k3_ready), k_in)

            load_x(Batch(0, 0, NB))
            sp.dma_start(cT_raw, cT.rearrange("(k p) b -> p k b", p=P)).then_inc(mod_in, 16)
            wmod_by_row = wmod.rearrange("(k p) f -> p k f", p=P)
            sp.dma_start(wmod_raw[:, :, 0:2 * D], wmod_by_row[:, :, 0:2 * D]).then_inc(mod_in, 16)
            sp.dma_start(wdq_raw[0:QROWS], w_dq.rearrange("(k r) f -> r k f", k=2)).then_inc(weights_in, 16)
            sp.dma_start(wuq_raw[0:QROWS], w_uqT.rearrange("(k r) f -> r k f", k=2)).then_inc(weights_in, 16)
            for k in range(2):
                half = slice(k * C, (k + 1) * C)
                sp.dma_start(wdkv_raw[:, :, half], w_dkvT.rearrange("(k p) c -> p k c", p=P)).then_inc(weights_in, 16)
                sp.dma_start(wuk_raw[half, :], w_ukT).then_inc(weights_in, 16)
                sp.dma_start(wuv_raw[half, :], w_uvT).then_inc(weights_in, 16)
            sp.dma_start(wmod_raw[:, :, 2 * D:6 * D], wmod_by_row[:, :, 2 * D:6 * D]).then_inc(mod_rest_in, 16)
            load_x(Batch(0, 1, NB))
            load_x(Batch(1, 0, NB))
            sp.dma_start(wout_raw, w_outT.rearrange("(k p) c -> p k c", p=P)).then_inc(ffn_in, 16)
            sp.dma_start(wa_raw, waT.rearrange("(k p) f -> p k f", p=P)).then_inc(ffn_in, 16)
            for k in range(2):
                half = slice(k * F // 2, (k + 1) * F // 2)
                sp.dma_start(wb_raw[k], wbT[half, :].rearrange("(k p) f -> p k f", p=P)).then_inc(ffn_in, 16)
            sp.dma_start(wg_raw, wgT.rearrange("(k p) f -> p k f", p=P)).then_inc(ffn_in, 16)
            sp.dma_start(bias_a[:], ba).then_inc(ffn_in, 16)
            sp.dma_start(bias_b[:], bb.to_broadcast([P, 2 * D])).then_inc(ffn_in, 16)

            def step(at):
                stack_q(at(1), 2)
                stack_q(at(0), 0)
                stack_q(at(0), 1)
                stack_k(at(0), 0)
                load_gates(at(2))
                prefetch_x(at(-1))
                load_maxima(at(1))
                stack_k(at(0), 1)
                store(at(4))
                stack_k(at(0), 2)

            pipeline(sp, step)
            for n in range(2):
                sp.wait_ge(stored[n], 16 * NB // 2)

        @block.tensor
        def _(pe):
            def product(outp, left, right, start, stop, **kw):
                pe.matmul(outp, left[0], right[0], start=start, stop=False, **kw)
                pe.matmul(outp, left[0], right[1], start=False, stop=False, **kw)
                return pe.matmul(outp, left[1], right[0], start=False, stop=stop, **kw)

            READERS = {
                "T1": ((h32_ready, 1, 1),), "Q": ((q1_ready, 1, 1), (qr_ready, 1, 1)), "CKV": ((ckv_ready, 1, 1),),
                "K": ((k1_ready, 1, 1), (kr_ready, 1, 1)), "V": ((v_ready, 1, 1),), "MT": ((mt_ready, 1, 1),),
                "PVa": ((o_ready, 2, 1),), "PVb": ((o_ready, 2, 2),), "OT0": ((attn_ready, 2, 1),), "OT1": ((attn_ready, 2, 2),),
                "AT": ((a_hi_ready, 1, 1), (a_lo_ready, 1, 1)), "OP": ((gated_ready, 1, 1),), "T2": ((g32_ready, 1, 1),),
                "GT": ((logit_rows_ready, 1, 1),), "GX": ((logits_ready, 1, 1),),
                "UP0": ((gelu_done, 2, 1),), "UP1": ((gelu_done, 2, 2),), "UP2": ((relu_done, 2, 1),), "UP3": ((relu_done, 2, 2),),
                "DN0": ((picked, 2, 1),), "DN1": ((picked, 2, 2),)}

            def bank_left(users):
                for user, b in users:
                    if not b.off:
                        for sem, a_batch, count in READERS[user]:
                            pe.wait_ge(sem, a_batch * b.n + count)
                        return

            def modulation(n):
                for w in range(2):
                    for f in range(KT):
                        block, col = w * KT + f, (3 * n + w) * D + f * P
                        for k in range(KT):
                            mm = pe.matmul(ps_t[:, n * 512 + block * NB:n * 512 + (block + 1) * NB], wmod_raw[:, k, col:col + P],
                                           c_silu[:, k, :], start=k == 0, stop=k == KT - 1)
                return mm

            def s_chunk(b, c):
                if b.off:
                    return
                if c == 0:
                    pe.wait_ge(q_in[b.parity], LOADS * (b.half + 1))
                    pe.wait_ge(k_in[b.parity], LOADS * (b.half + 1))
                if b.first and c == 0:
                    pe.wait_ge(clamp_ready, 3)
                    pe.wait_ge(modt_ready, 2)
                wait(pe, scores_out, CH * b.n + c)
                tile, heads = (0, range(8 * c, 8 * c + 8)) if c < 2 else (1, range(4 * c - 8, 4 * c - 4))
                width = P * (tile + 1)
                for n, h in enumerate(heads):
                    mm = pe.matmul(ps_s[:, n * width:(n + 1) * width], qs[b.parity][0:R, h, tile * P:(tile + 1) * P],
                                   ks[b.parity][0:R, h, 0:width], start=True, stop=True)
                mm.then_inc(s_done, 1)

            def st_chunk(b, c):
                if b.off:
                    return
                if b.first and c == 0:
                    pe.wait_ge(ones_ready, 2)
                if c == 0:
                    pe.wait_ge(maxrows_in, 16 * (b.n + 1))
                wait(pe, exp_done, CH * b.n + c)
                tile, h0, n = ST[c]
                width = S - P * tile
                for h in range(n):
                    mm = pe.matmul(ps_t[:, h * width:(h + 1) * width], ks[b.parity][0:RM, h0 + h, tile * P:(tile + 1) * P],
                                   qs[b.parity][0:RM, h0 + h, tile * P:S], start=True, stop=True)
                mm.then_inc(st_done, 1)

            def values(b, g, *users):
                if b.off:
                    return
                if g == 0:
                    pe.wait_ge(v_ready, b.n + 1)
                pe.wait_ge(masked, CH * b.n + ST_OF_GROUP[g])
                bank_left(users)
                for n in range(4):
                    h = 4 * g + n
                    dst = BANK["PVa"][32 * n:32 * n + HD + 1, (g % 2) * S:(g % 2 + 1) * S]
                    pe.matmul(dst, v[b.parity][:, 0, h, :], p0[:, h, :], start=True, stop=False)
                    mm = pe.matmul(dst[:, P:S], v[b.parity][:, 1, h, :], p1[:, h, :], start=False, stop=True)
                mm.then_inc(pv_done, 1)

            def turn_values(b, t, *users):
                if b.off:
                    return
                pe.wait_ge(o_ready, 2 * (b.n + 1))
                bank_left(users)
                for g in range(4):
                    mm = pe.transpose(BANK[f"OT{t}"][:, g * P:(g + 1) * P], oT[:, g, t * P:(t + 1) * P], ident[:])
                mm.then_inc(ot_done, 1)

            def turn(dst, src, done):
                for k in range(KT):
                    for t in range(TT):
                        mm = pe.transpose(dst[:, k * S + t * P:k * S + (t + 1) * P], src[:, t, k * P:(k + 1) * P], ident[:])
                mm.then_inc(done, 1)

            def turn_z1(b, *users):
                if b.off or b.first:
                    return
                pe.wait_ge(z1_ready, b.n + 1)
                bank_left(users)
                turn(BANK["T1"], z1, t1_done)

            def turn_attn(b, *users):
                if b.off:
                    return
                pe.wait_ge(attn_ready, 2 * (b.n + 1))
                bank_left(users)
                turn(BANK["AT"], attn, at_done)

            def turn_z2(b, *users):
                if b.off:
                    return
                pe.wait_ge(z2_ready, b.n + 1)
                bank_left(users)
                turn(BANK["T2"], z2, t2_done)

            def turn_maxima(b, *users):
                if b.off:
                    return
                pe.wait_ge(max_split, 4 * (b.n + 1))
                bank_left(users)
                wait_alone(pe)
                for t in range(TT):
                    mm = pe.transpose(mt_out[:, t * P:(t + 1) * P], mx_parts[:, t, :, :].rearrange("p c h -> p (c h)"), ident_b[:])
                mm.then_inc(mt_done, 1)

            def project_q(b, *users):
                if b.off:
                    return
                pe.wait_ge(h_hi_ready, b.n + 1)
                pe.wait_ge(h_lo_ready, b.n + 1)
                bank_left(users)
                for n in range(KT):
                    for k in range(KT):
                        cols = slice(n * P, (n + 1) * P)
                        mm = product(BANK["Q"][:, n * S:(n + 1) * S], (wq[0][:, k, cols], wq[1][:, k, cols]),
                                     (h_hi[:, k, :], h_lo[:, k, :]), k == 0, k == KT - 1)
                mm.then_inc(q_done, 1)

            def compress(b, *users):
                if b.off:
                    return
                pe.wait_ge(h_hi_ready, b.n + 1)
                pe.wait_ge(h_lo_ready, b.n + 1)
                bank_left(users)
                for k in range(KT):
                    mm = product(BANK["CKV"][:, 0:S], (wdkv[0][:, k, :], wdkv[1][:, k, :]), (h_hi[:, k, :], h_lo[:, k, :]),
                                 k == 0, k == KT - 1)
                mm.then_inc(ckv_done, 1)

            def expand_k(b, *users):
                if b.off:
                    return
                pe.wait_ge(ckv_ready, b.n + 1)
                bank_left(users)
                for n in range(KT):
                    for w in range(2):
                        mm = pe.matmul(BANK["K"][:, n * S:(n + 1) * S], wuk[w][:, n * P:(n + 1) * P], ckv[:], start=w == 0, stop=w == 1)
                mm.then_inc(k_done, 1)

            def expand_v(b, *users):
                if b.off:
                    return
                pe.wait_ge(ckv_ready, b.n + 1)
                bank_left(users)
                for t in range(TT):
                    for w in range(2):
                        mm = pe.matmul(BANK["V"][:, t * D:(t + 1) * D], ckv[:, t * P:(t + 1) * P], wuv[w][:], start=w == 0, stop=w == 1)
                mm.then_inc(v_done, 1)

            def project_out(b, *users):
                if b.off:
                    return
                pe.wait_ge(a_hi_ready, b.n + 1)
                pe.wait_ge(a_lo_ready, b.n + 1)
                if b.first:
                    pe.wait_ge(w_lo, BACK_SPLITS)
                bank_left(users)
                for t in range(TT):
                    tok = slice(t * P, (t + 1) * P)
                    for k in range(KT):
                        mm = product(BANK["OP"][:, t * D:(t + 1) * D], (a_hi[:, k, tok], a_lo[:, k, tok]),
                                     (wout[0][:, k, :], wout[1][:, k, :]), k == 0, k == KT - 1)
                mm.then_inc(op_done, 1)

            def gate(b, *users):
                if b.off:
                    return
                pe.wait_ge(g_hi_ready, b.n + 1)
                pe.wait_ge(g_lo_ready, b.n + 1)
                if b.first:
                    pe.wait_ge(w_lo, ALL_SPLITS)
                bank_left(users)
                for k in range(KT):
                    mm = product(BANK["GT"][0:2, 0:S], (wg[0][:, k, :], wg[1][:, k, :]), (g_hi[:, k, :], g_lo[:, k, :]), k == 0, k == KT - 1)
                mm.then_inc(gate_done, 1)

            def turn_gate(b, *users):
                if b.off:
                    return
                pe.wait_ge(logit_rows_ready, b.n + 1)
                bank_left(users)
                wait_alone(pe)
                for t in range(TT):
                    mm = pe.transpose(BANK["GX"][:, 2 * t:2 * t + 2], logit_rows[:, t * P:(t + 1) * P], ident[0:2, 0:2])
                mm.then_inc(gate_turned, 1)

            def up(b, u, *users):
                if b.off:
                    return
                pe.wait_ge(g_hi_ready, b.n + 1)
                pe.wait_ge(g_lo_ready, b.n + 1)
                if b.first:
                    pe.wait_ge(w_lo, ALL_SPLITS)
                bank_left(users)
                for n in range(2):
                    cols = slice((2 * u + n) * P, (2 * u + n + 1) * P)
                    for k in range(KT):
                        mm = product(BANK[f"UP{u}"][:, n * S:(n + 1) * S], (wa[0][:, k, cols], wa[1][:, k, cols]),
                                     (g_hi[:, k, :], g_lo[:, k, :]), k == 0, k == KT - 1)
                mm.then_inc(up_done, 1)

            def down(b, t, e, *users):
                if b.off:
                    return
                pe.wait_ge(hid_hi_ready, 4 * b.n + 2 * e + 2)
                pe.wait_ge((lo_gelu_ready, lo_relu_ready)[e], 2 * (b.n + 1))
                bank_left(users)
                dst = BANK[f"DN{t}"][:, e * D:(e + 1) * D]
                tok = slice(t * P, (t + 1) * P)
                for n in range(e * FT // 2, (e + 1) * FT // 2):
                    mm = product(dst, (hid_hi[:, n, tok], hid_lo[:, n, tok]), (wb[0][:, n, :], wb[1][:, n, :]),
                                 n == e * FT // 2, n == (e + 1) * FT // 2 - 1)
                mm.then_inc(dn_done, 1)

            pe.wait_ge(mod_in, 32)
            pe.wait_ge(silu_ready, 1)
            modulation(0).then_inc(mod_done, 1)
            pe.wait_ge(weights_in, 16 * 8)
            for n in range(KT):
                for k in range(2):
                    mm = pe.matmul(ps_c[:, n * D:(n + 1) * D], wdq_raw[0:QROWS, k, n * P:(n + 1) * P], wuq_raw[0:QROWS, k, :],
                                   start=k == 0, stop=k == 1)
            mm.then_inc(wq_done, 1)
            pe.wait_ge(consts_ready, 3)
            pe.wait_ge(blank, 4)
            pe.wait_ge(z1_ready, 1)
            turn(BANK["T1"], z1, t1_done)
            pe.wait_ge(mod_rest_in, 16)
            modulation(1)
            for n in range(2):
                for k in range(KT):
                    mm = pe.matmul(ps_s[0:NB, n * D:(n + 1) * D], c_silu[:, k, :], wmod_raw[:, k, (3 * n + 2) * D:(3 * n + 3) * D],
                                   start=k == 0, stop=k == KT - 1)
            mm.then_inc(mod_done, 1)
            pe.wait_ge(w_lo, FRONT_SPLITS)

            def step(at):
                turn_maxima(at(2), ("UP0", at(4)), ("Q", at(1)))
                turn_values(at(3), 0, ("PVb", at(3)))
                turn_values(at(3), 1, ("K", at(1)), ("CKV", at(1)), ("GX", at(5)))
                up(at(4), 2, ("MT", at(2)), ("UP0", at(4)))
                expand_v(at(1), ("OT0", at(3)), ("PVb", at(3)), ("PVa", at(3)), ("DN0", at(5)), ("UP3", at(5)), ("V", at(2)))
                gate(at(4), ("UP1", at(4)))
                turn_attn(at(3), ("OT1", at(3)))
                st_chunk(at(2), 0)
                up(at(4), 3, ("V", at(1)), ("OT0", at(3)), ("PVb", at(3)), ("PVa", at(3)), ("DN0", at(5)))
                project_out(at(3), ("UP2", at(4)), ("MT", at(2)))
                s_chunk(at(1), 0)
                st_chunk(at(2), 1)
                turn_z1(at(0), ("GT", at(4)), ("UP1", at(4)), ("DN1", at(5)), ("T1", at(1)))
                turn_gate(at(4), ("AT", at(3)), ("OT1", at(3)), ("K", at(1)), ("CKV", at(1)), ("GX", at(5)))
                down(at(4), 0, 0, ("UP3", at(4)))
                s_chunk(at(1), 1)
                st_chunk(at(2), 2)
                down(at(4), 0, 1)
                s_chunk(at(1), 2)
                st_chunk(at(2), 3)
                down(at(4), 1, 0, ("T1", at(0)), ("GT", at(4)))
                s_chunk(at(1), 3)
                turn_z2(at(3), ("OP", at(3)))
                compress(at(0), ("GX", at(4)), ("AT", at(3)), ("OT1", at(3)), ("K", at(1)))
                st_chunk(at(2), 4)
                down(at(4), 1, 1)
                s_chunk(at(1), 4)
                project_q(at(0), ("T2", at(3)), ("OP", at(3)), ("UP2", at(4)), ("MT", at(2)), ("UP0", at(4)), ("Q", at(1)))
                st_chunk(at(2), 5)
                values(at(2), 0, ("DN0", at(4)), ("UP3", at(4)), ("V", at(1)))
                s_chunk(at(1), 5)
                values(at(2), 1)
                expand_k(at(0), ("CKV", at(0)))
                up(at(3), 0, ("Q", at(0)), ("T2", at(3)))
                values(at(2), 2, ("PVa", at(2)))
                values(at(2), 3)
                up(at(3), 1, ("DN1", at(4)), ("T1", at(0)))

            mt_out = BANK["MT"][0:3 * NH, 0:P].bitcast(BF16)
            pipeline(pe, step)

        @block.scalar
        def _(act):
            act.wait_ge(mod_in, 32)
            act.activation(c_silu, cT_raw, ACT.Silu).then_inc(silu_ready, 1)

            def high_parts(some):
                for n in some:
                    act.activation(splits[n][0], splits[n][2], ACT.Copy).then_inc(w_hi, 1)

            act.wait_ge(weights_in, 16 * 8)
            high_parts(range(3))
            act.wait_ge(wq_done, 1)
            high_parts(range(3, FRONT_SPLITS))

            def rest_of_weights(b):
                if not b.first:
                    return
                act.wait_ge(ffn_in, 16 * 7)
                high_parts(range(FRONT_SPLITS, ALL_SPLITS))

            def values_copy(b, half):
                if b.off:
                    return
                act.wait_ge(pv_done, 4 * b.n + 2 * half + 2)
                wait(act, ot_done, 2 * b.n)
                act.activation(oT[:, 2 * half:2 * half + 2, :], BANK["PVa"][:].rearrange("p (g s) -> p g s", g=2), ACT.Copy).then_inc(o_ready, 1)

            def second_expert(b, t):
                if b.off:
                    return
                act.wait_ge(dn_done, 4 * b.n + 2 * t + 2)
                act.wait_ge(choice_ready, b.n + 1)
                wait(act, out_ready, b.n)
                act.activation(y[:, t, :], BANK[f"DN{t}"][:, D:2 * D], ACT.Copy, scale=second[b.parity][:, t:t + 1]).then_inc(second_ready, 1)

            def modulate(dst, src, base, n, ready):
                for k in range(KT):
                    ins = act.activation(dst[:, k, :], src[:, k * S:(k + 1) * S], ACT.Identity,
                                         bias=modT[:, bass.ds(n, 1), base + k], scale=modT[:, bass.ds(n, 1), base + 2 + k])
                ins.then_inc(ready, 1)

            def modulate_1(b):
                if b.off:
                    return
                act.wait_ge(t1_done, b.n + 1)
                wait(act, h_hi_ready, b.n)
                wait(act, h_lo_ready, b.n)
                if b.first:
                    act.wait_ge(modt_ready, 1)
                modulate(h32, BANK["T1"], 0, b.n, h32_ready)

            def modulate_2(b):
                if b.off:
                    return
                act.wait_ge(t2_done, b.n + 1)
                wait(act, g_hi_ready, b.n)
                wait(act, g_lo_ready, b.n)
                if b.first:
                    act.wait_ge(modt_ready, 2)
                modulate(g32, BANK["T2"], 4, b.n, g32_ready)

            def attn_hi(b):
                if b.off:
                    return
                act.wait_ge(at_done, b.n + 1)
                wait(act, op_done, b.n)
                act.activation(a_hi[:].rearrange("p k s -> p (k s)"), BANK["AT"][:], ACT.Copy).then_inc(a_hi_ready, 1)

            def first_part(b, src, parts, done, rest_ready, stack_in, ready):
                if b.off:
                    return
                act.wait_ge(done, b.n + 1)
                wait(act, rest_ready, b.n)
                wait(act, stack_in[1 - b.parity], LOADS * (b.half + b.parity))
                act.activation(parts[:, 0, :], src[:], ACT.Copy).then_inc(ready, 1)

            def q_first(b):
                first_part(b, BANK["Q"], parts_q, q_done, qr_ready, q_in, q1_ready)

            def k_first(b):
                first_part(b, BANK["K"], parts_k, k_done, kr_ready, k_in, k1_ready)

            def ckv_hi(b):
                if b.off:
                    return
                act.wait_ge(ckv_done, b.n + 1)
                wait(act, k_done, b.n)
                wait(act, v_done, b.n)
                act.activation(ckv[:], BANK["CKV"][:, 0:S], ACT.Copy).then_inc(ckv_hi_ready, 1)

            def v_copy(b):
                if b.off:
                    return
                act.wait_ge(v_done, b.n + 1)
                wait(act, pv_done, 4 * (b.n - 1))
                act.activation(v[b.parity][:, :, :, 0:HD], BANK["V"][:].rearrange("p (t h e) -> p t h e", t=TT, h=NH), ACT.Copy).then_inc(v_ready, 1)

            def maxima_rows(b):
                if b.off:
                    return
                act.wait_ge(mt_done, b.n + 1)
                wait(act, maxrows_in, 16 * b.n)
                act.activation(mx_rows[:], BANK["MT"][0:3 * NH, 0:P].bitcast(BF16), ACT.Copy).then_inc(mt_ready, 1)

            def gelu(b, u):
                if b.off:
                    return
                act.wait_ge(up_done, 4 * b.n + u + 1)
                wait(act, hid_hi_ready, 4 * b.n - 1 + u)
                wait(act, lo_relu_ready, 2 * b.n - 1 + u)
                for n in range(2):
                    ins = act.activation(hid32[:, u, n, :], BANK[f"UP{u}"][:, n * S:(n + 1) * S], ACT.Gelu,
                                         bias=bias_a[:, 2 * u + n:2 * u + n + 1])
                ins.then_inc(gelu_done, 1)

            def scores_copy(b, c):
                if b.off:
                    return
                act.wait_ge(s_done, CH * b.n + c + 1)
                wait(act, max_done, CH * b.n + c - 1)
                act.activation(score_rows[c % 2][:], ps_s[:], ACT.Copy).then_inc(scores_out, 1)

            def exponentials(b, c):
                if b.off:
                    return
                act.wait_ge(st_done, CH * b.n + c + 1)
                wait(act, pv_done, 4 * (b.n - 1) + (2, 1, 2, 4, 3, 4)[c])
                if b.first and c == 0:
                    act.wait_ge(w_lo, ALL_SPLITS)
                tile, h0, n = ST[c]
                act.activation((p0, p1)[tile][:, h0:h0 + n, :], ps_t[:].rearrange("p (h s) -> p h s", h=n), ACT.Exp, scale=SCALE).then_inc(exp_done, 1)

            def step(at):
                gelu(at(4), 0)
                values_copy(at(3), 1)
                maxima_rows(at(2))
                gelu(at(4), 1)
                v_copy(at(1))
                attn_hi(at(3))
                exponentials(at(2), 0)
                scores_copy(at(1), 0)
                exponentials(at(2), 1)
                modulate_1(at(0))
                scores_copy(at(1), 1)
                exponentials(at(2), 2)
                scores_copy(at(1), 2)
                second_expert(at(4), 0)
                exponentials(at(2), 3)
                scores_copy(at(1), 3)
                modulate_2(at(3))
                exponentials(at(2), 4)
                ckv_hi(at(0))
                second_expert(at(4), 1)
                scores_copy(at(1), 4)
                q_first(at(0))
                exponentials(at(2), 5)
                scores_copy(at(1), 5)
                values_copy(at(2), 0)
                k_first(at(0))
                rest_of_weights(at(0))

            pipeline(act, step)

        @block.vector
        def _(dve):
            def stats(b, n):
                if b.off:
                    return
                st, mv, ve = ln_st[n], ln_mv[n], ln_ve[n]
                s_st, s_mv, s_ve, s_rs, s_z = ((st1, mv1, ve1, rs1, z1_ready), (st2, mv2, ve2, rs2, z2_ready))[n]
                if n == 0:
                    dve.wait_ge(x_in[b.parity], 16 * (b.half + 1))
                else:
                    dve.wait_ge(x1_ready, b.n + 1)
                wait(dve, s_mv, TT * b.n)
                wait(dve, s_rs, b.n)
                wait(dve, s_z, b.n)
                for t in range(TT):
                    dve.bn_stats(st[:, t, :], xs[:, bass.ds(TT * b.n + t, 1), :].rearrange("p a d -> p (a d)")).then_inc(s_st, 1)
                for t in range(TT):
                    dve.wait_ge(s_st, TT * b.n + t + 1)
                    wait_alone(dve)
                    dve.bn_aggr(mv[:, t, :], st[:, t, :]).then_inc(s_mv, 1)
                dve.wait_ge(s_mv, TT * (b.n + 1))
                dve.tensor_scalar(ve[:], mv[:, :, 1], EPS, None, ALU.add).then_inc(s_ve, 1)

            def normalise(b, n):
                if b.off:
                    return
                dst, ready, s_rs, turned = ((z1, z1_ready, rs1, t1_done), (z2, z2_ready, rs2, t2_done))[n]
                dve.wait_ge(s_rs, b.n + 1)
                wait(dve, turned, b.n)
                for t in range(TT):
                    ins = dve.tensor_scalar(dst[:, t, :], xs[:, bass.ds(TT * b.n + t, 1), :].rearrange("p a d -> p (a d)"),
                                            ln_mv[n][:, t, 0:1], ln_rs[n][:, t:t + 1], ALU.subtract, ALU.mult)
                ins.then_inc(ready, 1)

            def low_parts(some):
                for n in some:
                    hi, lo, src = splits[n]
                    dve.wait_ge(w_hi, n + 1)
                    dve.tensor_tensor(lo, src, hi.bitcast(F32), ALU.subtract).then_inc(w_lo, 1)

            def take_modulation(n):
                blocks = ps_t[:, n * 512:n * 512 + 2 * KT * NB].rearrange("p (w k b) -> p w k b", w=2, k=KT)
                by_batch = modT[:].rearrange("p b (u w k) -> p u w k b", u=2, w=2)
                dve.wait_ge(mod_done, n + 1)
                for w in range(2):
                    ins = dve.tensor_scalar(by_batch[:, n, w], blocks[:, w], float(w), None, ALU.add)
                ins.then_inc(modt_ready, 1)

            def rest_of_modulation(b):
                if not b.first:
                    return
                take_modulation(1)
                gate_rows = ps_s[0:NB, 0:2 * D]
                dve.tensor_scalar(sign, gate_rows, 0.0, 2.0, ALU.is_ge, ALU.mult).then_inc(clamp_ready, 1)
                dve.wait_ge(clamp_ready, 1)
                dve.tensor_scalar(sign, sign, -1.0, None, ALU.add).then_inc(clamp_ready, 1)
                dve.wait_ge(clamp_ready, 2)
                dve.tensor_tensor(clamped, gate_rows, sign, ALU.mult).then_inc(clamp_ready, 1)
                dve.wait_ge(clamp_ready, 3)
                dve.scalar_tensor_tensor(out=clamped, in0=clamped, scalar=LEAST_GATE, in1=sign, op0=ALU.max, op1=ALU.mult).then_inc(clamp_ready, 1)

            def late_low_part(b, n):
                if b.first:
                    low_parts((n,))

            dve.memset(neg_half[:], -0.5).then_inc(blank, 1)
            for n in range(2):
                dve.memset(v[n][:, :, :, HD:HD + 1], 1.0).then_inc(blank, 1)
            dve.memset(ps_o[:], 0.0).then_inc(blank, 1)
            stats(Batch(0, 0, NB), 0)
            take_modulation(0)
            normalise(Batch(0, 0, NB), 0)
            low_parts(range(FRONT_SPLITS))

            def row_max(b, c):
                if b.off:
                    return
                dve.wait_ge(scores_hidden, CH * b.n + c + 1)
                if c == 0:
                    wait(dve, max_split, 4 * b.n)
                if c < 2:
                    dst, n = mx[:, 0, 8 * c:8 * c + 8], 8
                else:
                    dst, n = mx[:, 1, 4 * c - 8:4 * c - 4], 4
                dve.tensor_reduce(dst, score_rows[c % 2][:].rearrange("p (h k) -> p h k", h=n), AX_X, ALU.max).then_inc(max_done, 1)

            def split_maxima(b):
                if b.off:
                    return
                dve.wait_ge(max_done, CH * (b.n + 1))
                wait(dve, mt_done, b.n)
                dve.tensor_scalar(mx_parts[:, :, 0, :], mx[:], -1.0, None, ALU.mult).then_inc(max_split, 1)
                dve.wait_ge(max_split, 4 * b.n + 1)
                dve.scalar_tensor_tensor(out=mx_rest[:], in0=mx[:], scalar=-1.0, in1=mx_parts[:, :, 0, :],
                                         op0=ALU.mult, op1=ALU.subtract).then_inc(max_split, 1)
                dve.wait_ge(max_split, 4 * b.n + 2)
                dve.tensor_copy(mx_parts[:, :, 1, :], mx_rest[:]).then_inc(max_split, 1)
                dve.wait_ge(max_split, 4 * b.n + 3)
                dve.tensor_tensor(mx_parts[:, :, 2, :], mx_rest[:], mx_parts[:, :, 1, :], ALU.subtract).then_inc(max_split, 1)

            def divide(b, t):
                if b.off:
                    return
                src = BANK[f"OT{t}"][:].rearrange("p (h e) -> p h e", h=NH)
                dve.wait_ge(ot_done, 2 * b.n + t + 1)
                dve.reciprocal(rden[:, t, :], src[:, :, HD]).then_inc(rden_ready, 1)
                dve.wait_ge(rden_ready, 2 * b.n + t + 1)
                wait(dve, at_done, b.n)
                dve.tensor_tensor(attn[:, t, :].rearrange("p (h e) -> p h e", h=NH), src[:, :, 0:HD],
                                  rden[:, t, :].unsqueeze(2).to_broadcast([P, NH, HD]), ALU.mult).then_inc(attn_ready, 1)

            def add_first_expert(b, t):
                if b.off:
                    return
                dve.wait_ge(second_ready, 2 * b.n + t + 1)
                dve.scalar_tensor_tensor(out=y[:, t, :], in0=BANK[f"DN{t}"][:, 0:D], scalar=first[b.parity][:, t:t + 1], in1=y[:, t, :],
                                         op0=ALU.mult, op1=ALU.add).then_inc(picked, 1)
                dve.wait_ge(picked, 2 * b.n + t + 1)
                dve.scalar_tensor_tensor(out=y[:, t, :], in0=bias_b[:, 0:D], scalar=first[b.parity][:, t:t + 1], in1=y[:, t, :],
                                         op0=ALU.mult, op1=ALU.add).then_inc(biased, 1)
                dve.wait_ge(biased, 2 * b.n + t + 1)
                dve.scalar_tensor_tensor(out=y[:, t, :], in0=bias_b[:, D:2 * D], scalar=second[b.parity][:, t:t + 1], in1=y[:, t, :],
                                         op0=ALU.mult, op1=ALU.add).then_inc(y_ready, 1)

            def part_rest(b, src, parts, rest, done, part_ready, rest_ready, third_ready):
                if b.off:
                    return
                dve.wait_ge(done, b.n + 1)
                dve.wait_ge(part_ready, b.n + 1)
                wait(dve, third_ready, b.n)
                dve.tensor_tensor(rest[:], src[:], parts[:, 0, :], ALU.subtract).then_inc(rest_ready, 1)

            def second_part(b, parts, rest, rest_ready, ready):
                if b.off:
                    return
                dve.wait_ge(rest_ready, b.n + 1)
                dve.tensor_copy(parts[:, 1, :], rest[:]).then_inc(ready, 1)

            def q_rest(b):
                part_rest(b, BANK["Q"], parts_q, rest_q, q_done, q1_ready, qr_ready, q3_ready)

            def k_rest(b):
                part_rest(b, BANK["K"], parts_k, rest_k, k_done, k1_ready, kr_ready, k3_ready)

            def q_second(b):
                second_part(b, parts_q, rest_q, qr_ready, q2_ready)

            def k_second(b):
                second_part(b, parts_k, rest_k, kr_ready, k2_ready)

            def attn_low(b):
                if b.off:
                    return
                dve.wait_ge(a_hi_ready, b.n + 1)
                wait(dve, op_done, b.n)
                dve.tensor_tensor(a_lo[:].rearrange("p k s -> p (k s)"), BANK["AT"][:], a_hi[:].rearrange("p k s -> p (k s)").bitcast(F32),
                                  ALU.subtract).then_inc(a_lo_ready, 1)

            def gate_attn(b):
                if b.off:
                    return
                dve.wait_ge(op_done, b.n + 1)
                dve.wait_ge(gates_in[b.parity], 16 * (b.half + 1))
                wait(dve, x1_ready, b.n)
                wait(dve, t2_done, b.n)
                for t in range(TT):
                    ins = dve.tensor_tensor(gated[:, t, :], BANK["OP"][:, t * D:(t + 1) * D], gates[b.parity][:, 0, :], ALU.mult)
                ins.then_inc(gated_ready, 1)

            def h_high(b):
                if b.off:
                    return
                dve.wait_ge(h32_ready, b.n + 1)
                wait(dve, q_done, b.n)
                wait(dve, ckv_done, b.n)
                dve.tensor_copy(h_hi[:], h32[:]).then_inc(h_hi_ready, 1)

            def ckv_low(b):
                if b.off:
                    return
                dve.wait_ge(ckv_hi_ready, b.n + 1)
                dve.tensor_tensor(ckv[C:2 * C, :], BANK["CKV"][C:2 * C, 0:S], ckv[C:2 * C, :].bitcast(F32), ALU.subtract).then_inc(ckv_ready, 1)

            def g_high(b):
                if b.off:
                    return
                dve.wait_ge(g32_ready, b.n + 1)
                wait(dve, up_done, 4 * b.n)
                wait(dve, gate_done, b.n)
                dve.tensor_copy(g_hi[:], g32[:]).then_inc(g_hi_ready, 1)

            def gate_copy(b):
                if b.off:
                    return
                dve.wait_ge(gate_done, b.n + 1)
                wait(dve, gate_turned, b.n)
                dve.tensor_copy(logit_rows[:], BANK["GT"][0:2, 0:S]).then_inc(logit_rows_ready, 1)

            def choose_expert(b):
                if b.off:
                    return
                dve.wait_ge(gate_turned, b.n + 1)
                wait(dve, y_ready, 2 * (b.n - 1))
                wait(dve, choice_ready, b.n)
                dve.tensor_copy(logits[:], BANK["GX"][:, 0:2 * TT].rearrange("p (t e) -> p t e", e=2)).then_inc(logits_ready, 1)
                dve.wait_ge(logits_ready, b.n + 1)
                dve.tensor_tensor(first[b.parity][:], logits[:, :, 0], logits[:, :, 1], ALU.is_ge).then_inc(first_ready, 1)
                dve.wait_ge(first_ready, b.n + 1)
                dve.tensor_scalar(second[b.parity][:], first[b.parity][:], -1.0, 1.0, ALU.mult, ALU.add).then_inc(choice_ready, 1)

            def relu(b, u):
                if b.off:
                    return
                dve.wait_ge(up_done, 4 * b.n + u + 1)
                dve.wait_ge(lo_gelu_ready, 2 * b.n + u - 1)
                dve.wait_ge(hid_hi_ready, 4 * b.n + u - 1)
                for n in range(2):
                    ins = dve.tensor_scalar(hid32[:, u - 2, n, :], BANK[f"UP{u}"][:, n * S:(n + 1) * S],
                                            bias_a[:, 2 * u + n:2 * u + n + 1], 0.0, ALU.add, ALU.max)
                ins.then_inc(relu_done, 1)

            def hidden_high(b, u):
                if b.off:
                    return
                if u < 2:
                    dve.wait_ge(gelu_done, 2 * b.n + u + 1)
                else:
                    dve.wait_ge(relu_done, 2 * b.n + u - 1)
                wait(dve, dn_done, 4 * b.n)
                dve.tensor_copy(hid_hi[:, 2 * u:2 * u + 2, :], hid32[:, u % 2, :, :]).then_inc(hid_hi_ready, 1)

            def hidden_low(b, u):
                if b.off:
                    return
                dve.wait_ge(hid_hi_ready, 4 * b.n + u + 1)
                dve.tensor_tensor(hid_lo[:, 2 * u:2 * u + 2, :], hid32[:, u - 2, :, :],
                                  hid_hi[:, 2 * u:2 * u + 2, :].bitcast(F32), ALU.subtract).then_inc(lo_relu_ready, 1)

            def first_stats(b):
                if not b.first:
                    stats(b, 0)

            def first_normalise(b):
                if not b.first:
                    normalise(b, 0)

            def step(at):
                q_second(at(1))
                rest_of_modulation(at(1))
                row_max(at(2), 4)
                row_max(at(2), 5)
                split_maxima(at(2))
                k_rest(at(1))
                hidden_high(at(4), 0)
                k_second(at(1))
                late_low_part(at(1), 4)
                divide(at(3), 0)
                hidden_high(at(4), 1)
                divide(at(3), 1)
                first_stats(at(0))
                relu(at(4), 2)
                attn_low(at(3))
                hidden_high(at(4), 2)
                relu(at(4), 3)
                gate_copy(at(4))
                first_normalise(at(0))
                gate_attn(at(3))
                hidden_high(at(4), 3)
                hidden_low(at(4), 2)
                hidden_low(at(4), 3)
                stats(at(3), 1)
                h_high(at(0))
                row_max(at(1), 0)
                late_low_part(at(1), 5)
                choose_expert(at(4))
                normalise(at(3), 1)
                row_max(at(1), 1)
                late_low_part(at(1), 6)
                row_max(at(1), 2)
                late_low_part(at(1), 7)
                add_first_expert(at(4), 0)
                g_high(at(3))
                row_max(at(1), 3)
                late_low_part(at(1), 8)
                add_first_expert(at(4), 1)
                ckv_low(at(0))
                q_rest(at(0))

            pipeline(dve, step)

        @block.gpsimd
        def _(pool):
            pool.memset(ident[:], 0.0).then_inc(consts_ready, 1)
            pool.wait_ge(consts_ready, 1)
            pool.affine_select(out=ident[:], in_=ident[:], compare_op=ALU.not_equal, fill=1.0, base=0,
                               pattern=[[-1, P]], channel_multiplier=1).then_inc(consts_ready, 1)
            pool.wait_ge(consts_ready, 2)
            pool.tensor_copy(ident_b[:], ident[:]).then_inc(consts_ready, 1)

            def inverse_deviation(b, n):
                if b.off:
                    return
                ve, rs = ln_ve[n], ln_rs[n]
                s_ve, s_rs, used = ((ve1, rs1, z1_ready), (ve2, rs2, z2_ready))[n]
                pool.wait_ge(s_ve, b.n + 1)
                wait(pool, used, b.n)
                pool.tensor_tensor(rs[:], ve[:], neg_half[:], ALU.pow).then_inc(s_rs, 1)

            def add_attn(b):
                if b.off:
                    return
                pool.wait_ge(gated_ready, b.n + 1)
                wait_alone(pool)
                rows = xs[:, bass.ds(TT * b.n, TT), :]
                pool.tensor_tensor(rows, gated[:], rows, ALU.add).then_inc(x1_ready, 1)

            def gate_ffn(b):
                if b.off:
                    return
                pool.wait_ge(y_ready, 2 * (b.n + 1))
                for t in range(TT):
                    ins = pool.tensor_tensor(y[:, t, :], y[:, t, :], gates[b.parity][:, 1, :], ALU.mult)
                ins.then_inc(scaled, 1)

            def add_ffn(b):
                if b.off:
                    return
                pool.wait_ge(scaled, b.n + 1)
                wait_alone(pool)
                rows = xs[:, bass.ds(TT * b.n, TT), :]
                pool.tensor_tensor(rows, y[:], rows, ALU.add).then_inc(out_ready, 1)

            def h_low(b):
                if b.off:
                    return
                pool.wait_ge(h_hi_ready, b.n + 1)
                pool.tensor_tensor(h_lo[:], h32[:], h_hi[:].bitcast(F32), ALU.subtract).then_inc(h_lo_ready, 1)

            def g_low(b):
                if b.off:
                    return
                pool.wait_ge(g_hi_ready, b.n + 1)
                pool.tensor_tensor(g_lo[:], g32[:], g_hi[:].bitcast(F32), ALU.subtract).then_inc(g_lo_ready, 1)

            def q_third(b):
                if b.off:
                    return
                pool.wait_ge(q2_ready, b.n + 1)
                pool.tensor_tensor(parts_q[:, 2, :], rest_q[:], parts_q[:, 1, :], ALU.subtract).then_inc(q3_ready, 1)

            def k_third(b):
                if b.off:
                    return
                pool.wait_ge(k2_ready, b.n + 1)
                pool.tensor_tensor(parts_k[:, 2, :], rest_k[:], parts_k[:, 1, :], ALU.subtract).then_inc(k3_ready, 1)

            def hidden_low(b, u):
                if b.off:
                    return
                pool.wait_ge(hid_hi_ready, 4 * b.n + u + 1)
                pool.tensor_tensor(hid_lo[:, 2 * u:2 * u + 2, :], hid32[:, u, :, :],
                                   hid_hi[:, 2 * u:2 * u + 2, :].bitcast(F32), ALU.subtract).then_inc(lo_gelu_ready, 1)

            def hide_scores(b, c):
                if b.off:
                    return
                n = 8 if c < 2 else 4
                pool.wait_ge(scores_out, CH * b.n + c + 1)
                wait_alone(pool)
                by_head = score_rows[c % 2][:].rearrange("p (h k) -> p h k", h=n)
                diag = by_head[:, :, 1024 // n - P:1024 // n]
                pool.affine_select(out=diag, in_=diag, compare_op=ALU.is_ge, fill=NEG, base=0,
                                   pattern=[[0, n], [-1, P]], channel_multiplier=1).then_inc(scores_hidden, 1)

            def hide(b, c):
                if b.off:
                    return
                tile, h0, n = ST[c]
                pool.wait_ge(exp_done, CH * b.n + c + 1)
                wait_alone(pool)
                diag = (p0, p1)[tile][:, h0:h0 + n, 0:P]
                pool.affine_select(out=diag, in_=diag, compare_op=ALU.is_ge, fill=0.0, base=0,
                                   pattern=[[0, n], [1, P]], channel_multiplier=-1).then_inc(masked, 1)

            pool.wait_ge(blank, 1)
            inverse_deviation(Batch(0, 0, NB), 0)
            pool.wait_ge(rs1, 1)
            for n in range(2):
                pool.memset(ks[n][R:RM, :, :], 1.0).then_inc(ones_ready, 1)
                pool.wait_ge(ones_ready, n + 1)

            def first_inverse(b):
                if not b.first:
                    inverse_deviation(b, 0)

            def step(at):
                hidden_low(at(4), 1)
                first_inverse(at(0))
                hide(at(2), 0)
                add_attn(at(3))
                hide_scores(at(1), 0)
                inverse_deviation(at(3), 1)
                hide_scores(at(1), 1)
                h_low(at(0))
                hide(at(2), 1)
                hide_scores(at(1), 2)
                hide(at(2), 2)
                hide_scores(at(1), 3)
                hide(at(2), 3)
                g_low(at(3))
                hide(at(2), 4)
                hide_scores(at(1), 4)
                hide(at(2), 5)
                hide_scores(at(1), 5)
                gate_ffn(at(4))
                add_ffn(at(4))
                q_third(at(0))
                k_third(at(0))
                hidden_low(at(3), 0)

            pipeline(pool, step)


def kernel(L0_attn_x, L0_attn_w_dq, L0_attn_w_uq, L0_attn_w_dkv, L0_attn_w_ukv, L0_attn_w_out, L0_ffn_Wg,
           L0_ffn_W0a, L0_ffn_b0a, L0_ffn_W0b, L0_ffn_b0b, L0_ffn_W1a, L0_ffn_b1a, L0_ffn_W1b, L0_ffn_b1b, L0_c, L0_wmod):
    import numpy as np
    import concourse.bacc as bacc
    from concourse.bass_utils import run_bass_kernel_spmd

    n = np.ascontiguousarray
    nh, hd = 16, 16
    w_uk, w_uv = np.split(np.asarray(L0_attn_w_ukv), 2, axis=0)

    def by_tile(w):
        return n(np.asarray(w).T.reshape(-1, nh // 2, 2, hd).transpose(0, 2, 3, 1).reshape(w.shape[1], nh * hd))

    arrays = {
        "x": n(L0_attn_x), "w_dq": n(L0_attn_w_dq), "w_uqT": by_tile(L0_attn_w_uq), "w_dkvT": n(np.asarray(L0_attn_w_dkv).T),
        "w_ukT": by_tile(w_uk), "w_uvT": n(w_uv.T), "w_outT": n(np.asarray(L0_attn_w_out).T), "wgT": n(np.asarray(L0_ffn_Wg).T),
        "waT": n(np.concatenate([np.asarray(L0_ffn_W0a), np.asarray(L0_ffn_W1a)], axis=0).T),
        "wbT": n(np.concatenate([np.asarray(L0_ffn_W0b), np.asarray(L0_ffn_W1b)], axis=1).T),
        "ba": n(np.concatenate([np.asarray(L0_ffn_b0a), np.asarray(L0_ffn_b1a)]).reshape(-1, P).T),
        "bb": n(np.concatenate([np.asarray(L0_ffn_b0b), np.asarray(L0_ffn_b1b)])[None, :]),
        "cT": n(np.asarray(L0_c).T), "wmod": n(L0_wmod),
    }
    nc = bacc.Bacc("TRN2", target_bir_lowering=False, num_devices=1, dynamic_dma_scratch_size=8192)
    aps = {k: nc.dram_tensor(k, a.shape, F32, kind="ExternalInput").ap() for k, a in arrays.items()}
    out = nc.dram_tensor("out", arrays["x"].shape, F32, kind="ExternalOutput").ap()
    block_kernel(nc, **aps, out=out)
    result = run_bass_kernel_spmd(nc, [arrays], core_ids=[0])
    return result.results[0]["out"]
```
